# Optimizing a Trainium2 kernel written in Bass

```python
import numpy as np
import jax
import jax.numpy as jnp

def _softmax(x, axis=-1):
    return jax.nn.softmax(x, axis=axis)

def _gelu(x):
    return jax.nn.gelu(x, approximate=True)

def _silu(x):
    return jax.nn.silu(x)

def _sigmoid(x):
    return jax.nn.sigmoid(x)

def _layernorm(x, axis=-1, eps=1e-05):
    m = jnp.mean(x, axis=axis, keepdims=True)
    v = jnp.var(x, axis=axis, keepdims=True)
    return (x - m) / jnp.sqrt(v + eps)

def _scatter_add(tgt, idx, src, axis=0):
    return tgt.at[idx].add(src)

def _segment_sum(src, seg, n):
    return jax.ops.segment_sum(src, seg, n)
kernel_name = 'mk_cond_seq_d2_seqx_r2_f8a922'

def setup_inputs(seed: int=0):
    np.random.seed(seed)
    _w = jnp.asarray

    def _rec_inputs():
        import jax
        import jax.numpy as jnp
        _rk = jax.random.key(seed)
        x = -0.0003929 + 0.9999 * jax.random.normal(jax.random.fold_in(_rk, 1), (2, 2048, 512), jnp.float32)
        _lenS = 2048 - jax.random.randint(jax.random.fold_in(_rk, 7), (2,), 0, max(1, 2048 // 4) + 1, jnp.int32)
        _lenS2 = 2048 - jax.random.randint(jax.random.fold_in(_rk, 8), (2,), 0, max(1, 2048 // 4) + 1, jnp.int32)
        cond_256 = -0.0209273 + 1.04763 * jax.random.normal(jax.random.fold_in(_rk, 11), (2, 128), jnp.float32)
        return (x, cond_256)
    x, cond_256 = _rec_inputs()

    def _L0_cond_setup():
        import jax, jax.numpy as jnp
        import numpy as np
        EPS = 1e-06

        def act_quant(x):
            scale = 127.0 / jnp.clip(jnp.max(jnp.abs(x), axis=-1, keepdims=True), 1e-05, None)
            return jnp.clip(jnp.round(x * scale), -128.0, 127.0) / scale

        def weight_quant(w):
            scale = 1.0 / jnp.clip(jnp.mean(jnp.abs(w)), 1e-05, None)
            return jnp.clip(jnp.round(w * scale), -1.0, 1.0) / scale
        key = jax.random.key(seed)
        k0, k1, k2, k3, k4 = jax.random.split(key, 5)
        B, S, D, FF, C = (4, 2048, 512, 2048, 128)
        return {'x': jax.random.normal(k0, (B, S, D), jnp.float32), 'cond': jax.random.normal(k1, (B, C), jnp.float32), 'norm_w': jax.random.normal(k2, (D, C), jnp.float32) * 0.02, 'up_w': jax.random.normal(k3, (2 * FF, D), jnp.float32) * 0.02, 'down_w': jax.random.normal(k4, (D, FF), jnp.float32) * 0.02}
    _L0_cond_all = _L0_cond_setup()
    _L0_cond_in = {k: v for k, v in _L0_cond_all.items() if k in ('norm_w', 'up_w', 'down_w')}
    del _L0_cond_all

    def _L1_cond_setup():
        import jax, jax.numpy as jnp
        import numpy as np
        DIM = 512
        BN = 128
        H = 128
        DELTA_SCALE = 0.1
        key = jax.random.key(seed)
        ks = jax.random.split(key, 10)
        B, L = (16, 1024)

        def init(k, shape, fan_in):
            bound = 1.0 / np.sqrt(fan_in)
            return jax.random.uniform(k, shape, jnp.float32, -bound, bound)
        return {'x': jax.random.normal(ks[0], (B, L, DIM), jnp.float32), 'h_lang': jax.random.normal(ks[1], (B, H), jnp.float32), 'Wd': init(ks[2], (BN, DIM), DIM), 'bd': init(ks[3], (BN,), DIM), 'Wu': init(ks[4], (DIM, BN), BN), 'bu': init(ks[5], (DIM,), BN), 'Wdd': init(ks[6], (BN * DIM, H), H), 'bdd': init(ks[7], (BN * DIM,), H), 'Wdu': init(ks[8], (DIM * BN, H), H), 'bdu': init(ks[9], (DIM * BN,), H)}
    _L1_cond_all = _L1_cond_setup()
    _L1_cond_in = {k: v for k, v in _L1_cond_all.items() if k in ('Wd', 'bd', 'Wu', 'bu', 'Wdd', 'bdd', 'Wdu', 'bdu')}
    del _L1_cond_all
    return {'x': x, 'cond_256': cond_256, 'L0_cond_norm_w': _L0_cond_in['norm_w'], 'L0_cond_up_w': _L0_cond_in['up_w'], 'L0_cond_down_w': _L0_cond_in['down_w'], 'L1_cond_Wd': _L1_cond_in['Wd'], 'L1_cond_bd': _L1_cond_in['bd'], 'L1_cond_Wu': _L1_cond_in['Wu'], 'L1_cond_bu': _L1_cond_in['bu'], 'L1_cond_Wdd': _L1_cond_in['Wdd'], 'L1_cond_bdd': _L1_cond_in['bdd'], 'L1_cond_Wdu': _L1_cond_in['Wdu'], 'L1_cond_bdu': _L1_cond_in['bdu']}

def reference(x, cond_256, L0_cond_norm_w, L0_cond_up_w, L0_cond_down_w, L1_cond_Wd, L1_cond_bd, L1_cond_Wu, L1_cond_bu, L1_cond_Wdd, L1_cond_bdd, L1_cond_Wdu, L1_cond_bdu):
    import jax
    import jax.numpy as jnp

    def _L0_cond_ref(x, cond, norm_w, up_w, down_w):
        import jax, jax.numpy as jnp
        import numpy as np
        EPS = 1e-06

        def act_quant(x):
            scale = 127.0 / jnp.clip(jnp.max(jnp.abs(x), axis=-1, keepdims=True), 1e-05, None)
            return jnp.clip(jnp.round(x * scale), -128.0, 127.0) / scale

        def weight_quant(w):
            scale = 1.0 / jnp.clip(jnp.mean(jnp.abs(w)), 1e-05, None)
            return jnp.clip(jnp.round(w * scale), -1.0, 1.0) / scale
        scale = cond @ norm_w.T + 1.0
        ms = jnp.mean(x * x, axis=-1, keepdims=True)
        h = x * (scale[:, None, :] * jax.lax.rsqrt(ms + EPS))
        u = h @ up_w.T
        val, gate = jnp.split(u, 2, axis=-1)
        h = val * jax.nn.gelu(gate, approximate=False)
        hq = h + jax.lax.stop_gradient(act_quant(h) - h)
        wq = down_w + jax.lax.stop_gradient(weight_quant(down_w) - down_w)
        y = hq @ wq.T
        return y + x

    def _L1_cond_ref(x, h_lang, Wd, bd, Wu, bu, Wdd, bdd, Wdu, bdu):
        import jax, jax.numpy as jnp
        import numpy as np
        DIM = 512
        BN = 128
        H = 128
        DELTA_SCALE = 0.1
        B, L, D = x.shape
        dWd = ((h_lang @ Wdd.T + bdd) * DELTA_SCALE).reshape(B, BN, D)
        dWu = ((h_lang @ Wdu.T + bdu) * DELTA_SCALE).reshape(B, D, BN)
        Wd_b = Wd + dWd
        Wu_b = Wu + dWu
        down = jax.nn.relu(jnp.einsum('bld,bnd->bln', x, Wd_b) + bd)
        up = jnp.einsum('bln,bdn->bld', down, Wu_b) + bu
        return x + up
    x = _L0_cond_ref(x, cond_256, L0_cond_norm_w, L0_cond_up_w, L0_cond_down_w)
    x = _L1_cond_ref(x, cond_256, L1_cond_Wd, L1_cond_bd, L1_cond_Wu, L1_cond_bu, L1_cond_Wdd, L1_cond_bdd, L1_cond_Wdu, L1_cond_bdu)
    return x

_drawn_inputs = setup_inputs


def setup_inputs(seed=0):
    import zlib

    import numpy as np

    out = dict(_drawn_inputs(seed))
    spreads = {}
    factors = {'L1_cond_bd': 5.074}
    for name, (base, spread) in spreads.items():
        noise = np.random.default_rng([zlib.crc32(name.encode()), seed]).standard_normal(out[name].shape)
        drawn = base * np.exp(spread * noise) if base else spread * noise
        out[name] = jnp.asarray(drawn.astype(out[name].dtype))
    for name, factor in factors.items():
        out[name] = (out[name] * factor).astype(out[name].dtype)
    return out
```

```python
from contextlib import ExitStack

import numpy as np

import concourse.bass as bass
from concourse import mybir
from concourse.alu_op_type import AluOpType as ALU

F32 = mybir.dt.float32
F16 = mybir.dt.float16
F8 = mybir.dt.float8e4
I32 = mybir.dt.int32
ACT = mybir.ActivationFunctionType
AX_X = mybir.AxisListType.X
AR = bass.bass_isa.ReduceOp

P = 128
B, S, D = 2, 2048, 512
FF = 2048
H = 128
BN = 128
TB = 512
NB = B * S // TB
BPB = S // TB
KD = D // P
NP = FF // P
UW = 2 * P
QG = 4

EPS_RMS = 1e-6
EPS_QUANT = 1e-5
DELTA_SCALE = 0.1
ROUND = 1.5 * 2.0 ** 23
EXP_MASK = 0x7F800000
RSQRT_SEED = 0x5F3759DF
U_EXP, X_EXP = 14, 9

NG_HALF = BN * D // (4 * 512)
NG = 2 * NG_HALF

STEPS = NB * NP
DW_FIRST, DW_LAST = 4, 50
ASSEMBLE = DW_LAST + 1


def groups_of_step(p):
    n = DW_LAST - DW_FIRST + 1
    if not DW_FIRST <= p <= DW_LAST:
        return range(0)
    at = p - DW_FIRST
    return range(at * NG // n, (at + 1) * NG // n)


def adapter_step(i):
    return {0: 52, 1: 60}.get(i, (i + 2) * NP + 2)


STAT_PAIR = 10


def aux_plan():
    uses = [("scale", 0), ("stat", 0), ("rs", 0)]
    for p in range(STEPS):
        i, j = divmod(p, NP)
        uses += [("dw", g) for g in groups_of_step(p)]
        if j == STAT_PAIR and i + 1 < NB:
            uses.append(("stat", i + 1))
        for n in range(NB):
            if p == adapter_step(n):
                uses.append(("mid", n))
            if p == adapter_step(n) + 1:
                uses += [("up", n, k) for k in range(KD)]
        if j == NP - 2 and i + 1 < NB:
            uses.append(("rs", i + 1))
        if j == NP - 1:
            if i > 0:
                uses += [("y", i - 1, k) for k in range(KD)]
    uses += [("mid", NB - 2)] + [("up", NB - 2, k) for k in range(KD)]
    uses += [("y", NB - 1, k) for k in range(KD)]
    uses += [("mid", NB - 1)] + [("up", NB - 1, k) for k in range(KD)]
    return {key: n for n, key in enumerate(uses)}


def build(nc, x, cond, norm_w, up_w, down_w, Wd, bd, Wu, bu, Wdd, bdd, Wdu, bdu, out):
    aux = aux_plan()
    aux_keys = list(aux)
    with ExitStack() as ctx:
        def sb(name, shape, dt=F32):
            return ctx.enter_context(nc.sbuf_tensor(name, shape, dt))

        def sem(name):
            return ctx.enter_context(nc.semaphore(name))

        u_hi = sb("u_hi", [P, NP, KD, UW], F16)
        u_lo = sb("u_lo", [P, NP, KD, UW], F16)
        wq = sb("wq", [P, NP, D], F8)
        x_sb = sb("x_sb", [P, 4, KD, TB])
        x_hi = sb("x_hi", [P, KD, TB], F16)
        x_lo = sb("x_lo", [P, KD, TB], F16)
        h_sb = sb("h_sb", [P, NP, TB])
        q_sb = sb("q_sb", [P, NP, TB], F16)
        w_ring = sb("w_ring", [P, 4, 1024])
        gelu = sb("gelu", [P, 2, TB])
        tmp = sb("tmp", [P, 2, TB])
        work = sb("work", [P, TB])
        stage = sb("stage", [P, 2, TB])
        l1_wd = sb("l1_wd", [P, B, KD, BN])
        l1_wu = sb("l1_wu", [P, B, D])
        mid = sb("mid", [P, TB])
        hmax = sb("hmax", [P, TB])
        hmax_b = sb("hmax_b", [P, TB])
        qscale = sb("qscale", [P, TB])
        ident = sb("ident", [P, P])
        ones = sb("ones", [P, 1])
        cond_sb = sb("cond_sb", [P, 32])
        bd_sb = sb("bd_sb", [P, 1])
        bu_sb = sb("bu_sb", [P, KD])
        cs = sb("cs", [P, KD, B])
        cs_max = sb("cs_max", [P, B])
        cs_all = sb("cs_all", [P, B])
        cs_pow = sb("cs_pow", [P, B])
        cs_mul = sb("cs_mul", [P, B])
        cs_x = sb("cs_x", [P, KD, B])
        um = sb("um", [P, NP])
        um_all = sb("um_all", [P, NP])
        um_pow = sb("um_pow", [P, NP])
        um_mul = sb("um_mul", [P, NP])
        unscale = sb("unscale", [P, B, NP])
        dabs = sb("dabs", [P, 8])
        dsum = sb("dsum", [P, 1])
        dsum_all = sb("dsum_all", [P, 1])
        wmean = sb("wmean", [P, 1])
        wmul = sb("wmul", [P, 1])
        ms = sb("ms", [P, KD])
        ms_half = sb("ms_half", [P, KD])
        rs = sb("rs", [P, 2, KD])
        rs_t = sb("rs_t", [P, KD])
        u_raw = q_sb[:, :, :].rearrange("p c t -> p (c t)").bitcast(F32).rearrange(
            "p (s k m) -> p s k m", s=4, k=KD)
        d_raw = x_sb[:, 3, :, :].rearrange("p (s c) t -> p s (c t)", s=2)
        norm_raw = stage[:, 0, :]

        up_ps = [ctx.enter_context(nc.psum_tensor(f"up_ps{n}", [P, TB], F32)) for n in range(4)]
        aux_ps = [ctx.enter_context(nc.psum_tensor(f"aux_ps{n}", [P, TB], F32)) for n in range(4)]

        def bank(*key):
            return aux_ps[aux[key] % 4]

        s_small = sem("s_small")
        s_u = [sem(f"s_u{n}") for n in range(4)]
        s_d = [sem(f"s_d{n}") for n in range(2)]
        s_w = [sem(f"s_w{n}") for n in range(4)]
        s_x = [sem(f"s_load_x{n}") for n in range(4)]
        s_move = [sem(f"s_move{n}") for n in range(2)]
        s_store = [sem(f"s_store{n}") for n in range(4)]
        s_zero = sem("s_zero")
        s_const = sem("s_const")
        s_gate = sem("s_gate")
        s_val = sem("s_val")
        s_aux = sem("s_aux")
        s_um = sem("s_um")
        s_uma = sem("s_uma")
        s_umul = sem("s_umul")
        s_uhi = sem("s_uhi")
        s_ulo = sem("s_ulo")
        s_cs = sem("s_cs")
        s_cm = sem("s_cm")
        s_cma = sem("s_cma")
        s_ms = sem("s_ms")
        s_sq = sem("s_sq")
        s_sqr = sem("s_sqr")
        s_rs = sem("s_rs")
        s_xs = sem("s_xs")
        s_xhi = sem("s_xhi")
        s_xlo = sem("s_xlo")
        s_gelu = sem("s_gelu")
        s_h = sem("s_h")
        s_gm = sem("s_gm")
        s_m = sem("s_m")
        s_ma = sem("s_ma")
        s_q = sem("s_q")
        s_x1 = sem("s_x1")
        s_relu = sem("s_relu")
        s_out = sem("s_out")
        s_dabs = sem("s_dabs")
        s_dsum = sem("s_dsum")
        s_dsuma = sem("s_dsuma")
        s_wq = sem("s_wq")
        s_stage = sem("s_stage")
        s_l1w = sem("s_l1w")
        s_chain = sem("s_chain")

        def aux_ready(eng, *key):
            eng.wait_ge(s_aux, aux[key] + 1)

        def reader_done(key):
            kind, i = key[:2]
            return {
                "scale": (s_cs, 1),
                "stat": (s_ms, i + 1),
                "rs": (s_xs, KD * (i + 1)),
                "dw": (s_stage, i + 1),
                "y": (s_x1, KD * i + key[-1] + 1),
                "mid": (s_relu, i + 1),
                "up": (s_out, KD * i + key[-1] + 1),
            }[kind]

        block = ctx.enter_context(nc.Block())

        @block.sync
        def _(sp):
            def load_u(j):
                if j >= 4:
                    sp.wait_ge(s_ulo, j - 3)
                sp.dma_start(u_raw[:, j % 4, :, :], up_w[j]).then_inc(s_u[j % 4], 16)

            def load_d(n):
                if 2 <= n < 10:
                    sp.wait_ge(s_dabs, n - 1)
                elif n >= 10:
                    sp.wait_ge(s_wq, n - 9)
                sp.dma_start(d_raw[:, n % 2, :], down_w[n % 8]).then_inc(s_d[n % 2], 16)

            def load_w(n):
                if n >= 4:
                    sp.wait_ge(s_aux, aux["dw", (n - 4) // 2] + 1)
                src = Wdd if n < NG else Wdu
                sp.dma_start(w_ring[:, n % 4, :], src[n % NG]).then_inc(s_w[n % 4], 16)

            def load_x(i):
                if i >= 4:
                    sp.wait_ge(s_store[i % 4], 16 * (i // 4))
                if i == 3:
                    sp.wait_ge(s_wq, 8)
                sp.dma_start(x_sb[:, i % 4, :, :], x[i]).then_inc(s_x[i % 4], 16)

            def store(i):
                sp.wait_ge(s_out, KD * (i + 1))
                sp.dma_start(out[i], x_sb[:, i % 4, :, :]).then_inc(s_store[i % 4], 16)

            sp.dma_start(norm_raw, norm_w).then_inc(s_small, 16)
            sp.wait_ge(s_zero, 1)
            sp.dma_start(cond_sb[:, 0:B], cond).then_inc(s_small, 16)
            sp.dma_start(bd_sb[:, :], bd).then_inc(s_small, 16)
            sp.dma_start(bu_sb[:, :], bu).then_inc(s_small, 16)
            load_u(0)
            load_x(0)
            load_u(1)
            load_u(2)
            for g in groups_of_step(DW_FIRST):
                load_w(2 * g)
                load_w(2 * g + 1)
            for p in range(STEPS):
                i, j = divmod(p, NP)
                if i == 0 and j + 3 < NP:
                    load_u(j + 3)
                if i == 0 and j % 2 == 0:
                    load_d(j // 2)
                if i == 1 and j < 8:
                    load_d(8 + j)
                if p >= DW_FIRST:
                    for g in groups_of_step(p + 1):
                        load_w(2 * g)
                        load_w(2 * g + 1)
                if p == DW_LAST:
                    for n, parts in ((2 * NG, (Wd, bdd)), (2 * NG + 1, (Wu, bdu))):
                        sp.wait_ge(s_aux, aux["dw", (n - 4) // 2] + 1)
                        for c, part in enumerate(parts):
                            sp.dma_start(w_ring[:, n % 4, 512 * c:512 * c + 512], part)\
                                .then_inc(s_w[n % 4], 16)
                for n in range(NB):
                    if p == adapter_step(n) + 3:
                        store(n)
                        if n == 0:
                            load_x(4)
                if j == 4 and i + 1 < NB and i + 1 != 4:
                    load_x(i + 1)
            for i in (NB - 2, NB - 1):
                store(i)
            for n in range(4):
                sp.wait_ge(s_store[n], 16 * (NB // 4))

        @block.gpsimd
        def _(pool):
            pool.memset(ones[:, :], 1.0).then_inc(s_const, 1)
            pool.memset(ident[:, :], 1.0).then_inc(s_const, 1)
            pool.wait_ge(s_const, 2)
            pool.affine_select(out=ident[:, :], in_=ident[:, :], compare_op=ALU.is_equal, fill=0.0,
                               base=0, pattern=[[-1, P]], channel_multiplier=1).then_inc(s_const, 1)

            def all_u(j):
                pool.wait_ge(s_um, j + 1)
                pool.partition_all_reduce(um_all[:, j:j + 1], um[:, j:j + 1], P, AR.absmax)\
                    .then_inc(s_uma, 1)

            pool.wait_ge(s_cm, 1)
            pool.partition_all_reduce(cs_all[:, :], cs_max[:, :], P, AR.absmax).then_inc(s_cma, 1)
            for j in range(NP):
                all_u(j)
            pool.wait_ge(s_m, 1)
            pool.partition_all_reduce(hmax_b[:, :], hmax[:, :], P, AR.absmax).then_inc(s_ma, 1)
            pool.wait_ge(s_dsum, 1)
            pool.partition_all_reduce(dsum_all[:, :], dsum[:, :], P, AR.add).then_inc(s_dsuma, 1)
            for i in range(1, NB):
                pool.wait_ge(s_m, i + 1)
                pool.partition_all_reduce(hmax_b[:, :], hmax[:, :], P, AR.absmax).then_inc(s_ma, 1)

        @block.scalar
        def _(act):
            def squares(i):
                act.wait_ge(s_x[i % 4], 16 * (i // 4 + 1))
                for k in range(KD):
                    n = (KD - 1) * i + k - 1
                    if k == 0:
                        if i:
                            act.wait_ge(s_gm, 2 * (i - 1) + 1)
                        dst = work[:, :]
                    else:
                        if k <= 2 and i:
                            act.wait_ge(s_xlo, KD * i)
                        if k > 2:
                            act.wait_ge(s_sqr, n - 1)
                        dst = tmp[:, k % 2, :]
                    act.activation(dst, x_sb[:, i % 4, k, :], ACT.Square).then_inc(s_sq, 1)

            def x_high(i):
                for k in range(KD):
                    act.wait_ge(s_xs, KD * i + k + 1)
                    act.activation(x_hi[:, k, :], tmp[:, k % 2, :], ACT.Copy).then_inc(s_xhi, 1)

            def u_high(j):
                act.wait_ge(s_umul, 3 * j + 1)
                act.activation(u_hi[:, j, :, :], u_raw[:, j % 4, :, :], ACT.Copy,
                               scale=um_mul[:, j:j + 1]).then_inc(s_uhi, 1)

            def down_abs(n):
                act.wait_ge(s_d[n % 2], 16 * (n // 2 + 1))
                act.activation(d_raw[:, n % 2, :], d_raw[:, n % 2, :], ACT.Abs,
                               accum_out=dabs[:, n:n + 1]).then_inc(s_dabs, 1)

            def stage_group(g):
                aux_ready(act, "dw", g)
                if g >= 2:
                    act.wait_ge(s_move[g % 2], 16 * B * (g // 2))
                act.activation(stage[:, g % 2, :], bank("dw", g)[:, :], ACT.Copy)\
                    .then_inc(s_stage, 1)
                act.wait_ge(s_stage, g + 1)
                for b in range(B):
                    rows = stage[b:b + 97:32, g % 2, :]
                    if g < NG_HALF:
                        dst = l1_wd[g:g + 97:32, b, :, :].rearrange("q k n -> q (k n)")
                    else:
                        dst = l1_wu[g - NG_HALF:g - NG_HALF + 97:32, b, :]
                    act.dma_start(dst, rows).then_inc(s_move[g % 2], 16)

            def adapter_relu(n):
                aux_ready(act, "mid", n)
                if n:
                    aux_ready(act, "up", n - 1, KD - 1)
                act.activation(mid[:, :], bank("mid", n)[:, :], ACT.Relu, bias=bd_sb[:, 0:1])\
                    .then_inc(s_relu, 1)

            squares(0)
            u_high(0)
            x_high(0)
            u_high(1)
            for p in range(STEPS):
                i, j = divmod(p, NP)
                act.wait_ge(s_gate, p + 1)
                if i == 0:
                    act.wait_ge(s_umul, 3 * (j + 1))
                if p >= 2:
                    act.wait_ge(s_h, p - 1)
                act.activation(gelu[:, p % 2, :], up_ps[2 * (p % 2)][:, :], ACT.Gelu,
                               scale=unscale[:, i // BPB, j:j + 1]).then_inc(s_gelu, 1)
                if i == 0 and j + 2 < NP:
                    u_high(j + 2)
                if i == 0 and j % 2 == 1:
                    down_abs(j // 2)
                if j > 0:
                    for g in groups_of_step(p - 1):
                        stage_group(g)
                if j == STAT_PAIR - 2 and i + 1 < NB:
                    squares(i + 1)
                for n in range(NB):
                    if p == adapter_step(n) + 1:
                        adapter_relu(n)
                if j == NP - 1 and i + 1 < NB:
                    x_high(i + 1)
                if j == NP - 1:
                    for g in groups_of_step(p):
                        stage_group(g)
            adapter_relu(NB - 2)
            adapter_relu(NB - 1)

        @block.tensor
        def _(pe):
            def take(*key):
                n = aux[key]
                if n >= 4:
                    pe.wait_ge(*reader_done(aux_keys[n - 4]))
                return aux_ps[n % 4]

            def up_half(p, half, sem_):
                i, j = divmod(p, NP)
                ps = up_ps[2 * (p % 2) + (1 - half)]
                cols = slice(P * half, P * half + P)
                for k in range(KD):
                    if j == 0 and half == 1:
                        pe.wait_ge(s_xhi, KD * i + k + 1)
                        pe.wait_ge(s_xlo, KD * i + k + 1)
                    whi, wlo = u_hi[:, j, k, cols], u_lo[:, j, k, cols]
                    pe.matmul(ps[:, :], whi, x_hi[:, k, :], start=(k == 0), stop=False)
                    pe.matmul(ps[:, :], whi, x_lo[:, k, :], start=False, stop=False)
                    mm = pe.matmul(ps[:, :], wlo, x_hi[:, k, :], start=False, stop=(k == KD - 1))
                mm.then_inc(sem_, 1)

            def pair(p):
                if p < NP:
                    pe.wait_ge(s_uhi, p + 1)
                    pe.wait_ge(s_ulo, p + 1)
                if p >= 2:
                    pe.wait_ge(s_gelu, p - 1)
                up_half(p, 1, s_gate)
                if p >= 2:
                    pe.wait_ge(s_h, p - 1)
                up_half(p, 0, s_val)

            def adapter_group(g):
                ps = take("dw", g)
                for q in range(4):
                    n = 2 * g + q // 2
                    if q % 2 == 0:
                        pe.wait_ge(s_w[n % 4], 16 * (n // 4 + 1))
                    mm = pe.matmul(ps[32 * q:32 * q + 32, :], cond_sb[:, :],
                                   w_ring[:, n % 4, 512 * (q % 2):512 * (q % 2) + 512],
                                   start=True, stop=True)
                mm.then_inc(s_aux, 1)

            def stat(i):
                ps = take("stat", i)
                pe.wait_ge(s_sqr, (KD - 1) * (i + 1))
                for t in range(TB // P):
                    mm = pe.matmul(ps[:, t:t + 1], work[:, P * t:P * t + P], ones[:, :],
                                   start=True, stop=True)
                mm.then_inc(s_aux, 1)

            def spread_rs(i):
                ps = take("rs", i)
                pe.wait_ge(s_rs, i + 1)
                for t in range(TB // P):
                    mm = pe.transpose(ps[:, P * t:P * t + P],
                                      rs[:, i % 2, t:t + 1].to_broadcast([P, P]), ident[:, :])
                mm.then_inc(s_aux, 1)

            def down(i, k):
                ps = take("y", i, k)
                if k == 0:
                    pe.wait_ge(s_q, NP * (i + 1))
                    pe.wait_ge(s_wq, 8)
                for c in range(NP):
                    mm = pe.matmul(ps[:, :], wq[:, c, P * k:P * k + P], q_sb[:, c, :],
                                   start=(c == 0), stop=(c == NP - 1))
                mm.then_inc(s_aux, 1)

            def last_down(i):
                banks = [take("y", i, k) for k in range(KD)]
                for c in range(NP):
                    pe.wait_ge(s_q, NP * i + c + 1)
                    for k in range(KD):
                        mm = pe.matmul(banks[k][:, :], wq[:, c, P * k:P * k + P], q_sb[:, c, :],
                                       start=(c == 0), stop=(c == NP - 1))
                        if c == NP - 1:
                            mm.then_inc(s_aux, 1)

            def adapter_mid(i):
                ps = take("mid", i)
                pe.wait_ge(s_l1w, 4)
                for k in range(KD):
                    pe.wait_ge(s_x1, KD * i + k + 1)
                    mm = pe.matmul(ps[:, :], l1_wd[:, i // BPB, k, :], x_sb[:, i % 4, k, :],
                                   start=(k == 0), stop=(k == KD - 1))
                mm.then_inc(s_aux, 1)

            def adapter_up(i):
                pe.wait_ge(s_relu, i + 1)
                for k in range(KD):
                    ps = take("up", i, k)
                    pe.matmul(ps[:, :], l1_wu[:, i // BPB, P * k:P * k + P], mid[:, :],
                              start=True, stop=True).then_inc(s_aux, 1)

            pe.wait_ge(s_const, 3)
            pe.wait_ge(s_small, 64)
            ps = take("scale", 0)
            for k in range(KD):
                mm = pe.matmul(ps[:, B * k:B * k + B], norm_raw[:, P * k:P * k + P],
                               cond_sb[:, 0:B], start=True, stop=True)
            mm.then_inc(s_aux, 1)
            stat(0)
            spread_rs(0)
            for p in range(STEPS):
                i, j = divmod(p, NP)
                pair(p)
                for g in groups_of_step(p):
                    adapter_group(g)
                if j == STAT_PAIR and i + 1 < NB:
                    stat(i + 1)
                for n in range(NB):
                    if p == adapter_step(n):
                        adapter_mid(n)
                    if p == adapter_step(n) + 1:
                        adapter_up(n)
                if j == NP - 2 and i + 1 < NB:
                    spread_rs(i + 1)
                if j == NP - 1:
                    if i > 0:
                        for k in range(KD):
                            down(i - 1, k)
            adapter_mid(NB - 2)
            adapter_up(NB - 2)
            last_down(NB - 1)
            adapter_mid(NB - 1)
            adapter_up(NB - 1)

        @block.vector
        def _(dve):
            links = [0]

            def link(ins):
                ins.then_inc(s_chain, 1)
                links[0] += 1
                dve.wait_ge(s_chain, links[0])

            def power_of_two(pow_, mul, top, exp, last):
                link(dve.tensor_scalar(mul, top, 1e-30, None, ALU.max))
                link(dve.tensor_scalar(pow_.bitcast(I32), mul.bitcast(I32), EXP_MASK, None,
                                       ALU.bitwise_and))
                ins = dve.tensor_scalar(mul.bitcast(I32), pow_.bitcast(I32), -1.0,
                                        float((254 + exp) * 2 ** 23), ALU.mult, ALU.add)
                last(ins)

            def u_max(j):
                dve.wait_ge(s_u[j % 4], 16 * (j // 4 + 1))
                dve.tensor_reduce(um[:, j:j + 1],
                                  u_raw[:, j % 4, :, :].rearrange("p k m -> p (k m)"), AX_X,
                                  ALU.max, apply_absolute_value=True).then_inc(s_um, 1)

            def u_scale(j):
                dve.wait_ge(s_uma, j + 1)
                power_of_two(um_pow[:, j:j + 1], um_mul[:, j:j + 1], um_all[:, j:j + 1], U_EXP,
                             lambda ins: ins.then_inc(s_umul, 1))
                for b in range(B):
                    dve.tensor_scalar(unscale[:, b, j:j + 1], um_pow[:, j:j + 1],
                                      2.0 ** -(U_EXP + X_EXP), cs_pow[:, b:b + 1],
                                      ALU.mult, ALU.mult).then_inc(s_umul, 1)

            def u_low(j):
                dve.wait_ge(s_uhi, j + 1)
                dve.wait_ge(s_umul, 3 * j + 1)
                flat = lambda t: t.rearrange("p k m -> p (k m)")
                dve.scalar_tensor_tensor(out=flat(u_lo[:, j, :, :]),
                                         in0=flat(u_raw[:, j % 4, :, :]),
                                         scalar=um_mul[:, j:j + 1], in1=flat(u_hi[:, j, :, :]),
                                         op0=ALU.mult, op1=ALU.subtract).then_inc(s_ulo, 1)

            def condition():
                aux_ready(dve, "scale", 0)
                ins = dve.tensor_scalar(cs[:, :, :].rearrange("p k b -> p (k b)"),
                                        bank("scale", 0)[:, 0:KD * B], 1.0, None, ALU.add)
                ins.then_inc(s_cs, 1)
                dve.wait_ge(s_cs, 1)
                dve.tensor_reduce(cs_max[:, :], cs[:, :, :].rearrange("p k b -> p b k"), AX_X,
                                  ALU.max, apply_absolute_value=True).then_inc(s_cm, 1)

            def condition_scale():
                dve.wait_ge(s_cma, 1)
                power_of_two(cs_pow[:, :], cs_mul[:, :], cs_all[:, :], X_EXP, link)
                for b in range(B):
                    link(dve.tensor_scalar(cs_x[:, :, b], cs[:, :, b], cs_mul[:, b:b + 1], None,
                                           ALU.mult))

            def add_squares(i):
                for k in range(1, KD):
                    dve.wait_ge(s_sq, KD * i + k + 1)
                    n = (KD - 1) * i + k
                    if k > 1:
                        dve.wait_ge(s_sqr, n - 1)
                    dve.tensor_tensor(work[:, :], work[:, :], tmp[:, k % 2, :], ALU.add)\
                        .then_inc(s_sqr, 1)

            def rsqrt(i):
                aux_ready(dve, "stat", i)
                ins = dve.tensor_scalar(ms[:, :], bank("stat", i)[:, 0:TB // P], 1.0 / D, EPS_RMS,
                                        ALU.mult, ALU.add)
                ins.then_inc(s_ms, 1)
                dve.wait_ge(s_ms, i + 1)
                y = rs[:, i % 2, :]
                link(dve.tensor_scalar(ms_half[:, :], ms[:, :], -0.5, None, ALU.mult))
                link(dve.tensor_scalar(rs_t[:, :].bitcast(I32), ms[:, :].bitcast(I32), 1, None,
                                       ALU.logical_shift_right))
                link(dve.tensor_scalar(y.bitcast(I32), rs_t[:, :].bitcast(I32), -1.0,
                                       float(RSQRT_SEED), ALU.mult, ALU.add))
                for n in range(4):
                    link(dve.tensor_tensor(rs_t[:, :], y, y, ALU.mult))
                    link(dve.tensor_tensor(rs_t[:, :], rs_t[:, :], ms_half[:, :], ALU.mult))
                    ins = dve.scalar_tensor_tensor(out=y, in0=rs_t[:, :], scalar=1.5, in1=y,
                                                   op0=ALU.add, op1=ALU.mult)
                    if n < 3:
                        link(ins)
                ins.then_inc(s_rs, 1)

            def prepare(i):
                aux_ready(dve, "rs", i)
                dve.wait_ge(s_sqr, (KD - 1) * (i + 1))
                if i:
                    dve.wait_ge(s_val, NP * i)

                def low(k):
                    dve.wait_ge(s_xhi, KD * i + k + 1)
                    dve.wait_ge(s_xs, KD * i + k + 1)
                    dve.tensor_tensor(x_lo[:, k, :], tmp[:, k % 2, :], x_hi[:, k, :],
                                      ALU.subtract).then_inc(s_xlo, 1)

                for k in range(KD):
                    if k >= 2:
                        dve.wait_ge(s_xlo, KD * i + k - 1)
                    ins = dve.scalar_tensor_tensor(
                        out=tmp[:, k % 2, :], in0=bank("rs", i)[:, :],
                        scalar=cs_x[:, k, i // BPB:i // BPB + 1], in1=x_sb[:, i % 4, k, :],
                        op0=ALU.mult, op1=ALU.mult)
                    ins.then_inc(s_xs, 1)
                    if k >= 1:
                        low(k - 1)
                low(KD - 1)

            def multiply(p):
                i, j = divmod(p, NP)
                dve.wait_ge(s_val, p + 1)
                dve.wait_ge(s_gelu, p + 1)
                if i == 0:
                    dve.wait_ge(s_umul, 3 * (j + 1))
                else:
                    dve.wait_ge(s_q, p + 1 - NP)
                dve.scalar_tensor_tensor(out=h_sb[:, j, :], in0=up_ps[2 * (p % 2) + 1][:, :],
                                         scalar=unscale[:, i // BPB, j:j + 1],
                                         in1=gelu[:, p % 2, :], op0=ALU.mult, op1=ALU.mult)\
                    .then_inc(s_h, 1)

            def group_max(i, g):
                c = QG * g
                dve.wait_ge(s_h, NP * i + c + QG)
                src = h_sb[:, c:c + QG, :].rearrange("p c t -> p t c")
                if g == 0:
                    if i:
                        dve.wait_ge(s_ma, i)
                    link(dve.tensor_reduce(hmax[:, :], src, AX_X, ALU.max,
                                           apply_absolute_value=True))
                    return
                if g == 1 and i > 0:
                    dve.wait_ge(s_m, i)
                if g == 1 and i > 1:
                    dve.wait_ge(s_x1, KD * (i - 1))
                if g == 2 and i + 1 < NB:
                    aux_ready(dve, "stat", i + 1)
                link(dve.tensor_reduce(work[:, :], src, AX_X, ALU.max, apply_absolute_value=True))
                ins = dve.tensor_tensor(hmax[:, :], hmax[:, :], work[:, :], ALU.max)
                if g == NP // QG - 1:
                    ins.then_inc(s_m, 1)
                else:
                    ins.then_inc(s_gm, 1)
                    dve.wait_ge(s_gm, 2 * i + g)

            def scales(i):
                dve.wait_ge(s_ma, i + 1)
                link(dve.tensor_scalar(hmax_b[:, :], hmax_b[:, :], EPS_QUANT, None, ALU.max))
                link(dve.reciprocal(qscale[:, :], hmax_b[:, :]))
                link(dve.tensor_scalar(qscale[:, :], qscale[:, :], 127.0, None, ALU.mult))

            def y_scale(i):
                dve.wait_ge(s_m, min(i + 1, NB))
                if i == NB:
                    dve.wait_ge(s_x1, KD * (i - 1))
                link(dve.reciprocal(work[:, :], qscale[:, :]))
                link(dve.tensor_scalar(work[:, :], work[:, :], wmean[:, 0:1], None, ALU.mult))

            def quantise(i, c):
                if c == 0 and i:
                    aux_ready(dve, "y", i - 1, KD - 1)
                link(dve.tensor_tensor(h_sb[:, c, :], h_sb[:, c, :], qscale[:, :], ALU.mult))
                dve.tensor_scalar(q_sb[:, c, :], h_sb[:, c, :], ROUND, -ROUND, ALU.add, ALU.add)\
                    .then_inc(s_q, 1)

            def residual(i, k):
                aux_ready(dve, "y", i, k)
                ps = bank("y", i, k)
                link(dve.tensor_tensor(ps[:, :], ps[:, :], work[:, :], ALU.mult))
                dve.tensor_tensor(x_sb[:, i % 4, k, :], ps[:, :], x_sb[:, i % 4, k, :],
                                  ALU.add).then_inc(s_x1, 1)

            def finish(i, k):
                aux_ready(dve, "up", i, k)
                dve.scalar_tensor_tensor(out=x_sb[:, i % 4, k, :], in0=bank("up", i, k)[:, :],
                                         scalar=bu_sb[:, k:k + 1], in1=x_sb[:, i % 4, k, :],
                                         op0=ALU.add, op1=ALU.add).then_inc(s_out, 1)

            def down_mean():
                dve.wait_ge(s_dabs, 8)
                dve.tensor_reduce(dsum[:, :], dabs[:, :], AX_X, ALU.add).then_inc(s_dsum, 1)

            def down_scale():
                dve.wait_ge(s_dsuma, 1)
                link(dve.tensor_scalar(wmean[:, :], dsum_all[:, :], 1.0 / (D * FF), 1e-5,
                                       ALU.mult, ALU.max))
                link(dve.reciprocal(wmul[:, :], wmean[:, :]))

            def down_quantise(n):
                dve.wait_ge(s_d[n % 2], 16 * (4 + n // 2 + 1))
                raw = d_raw[:, n % 2, :]
                link(dve.tensor_scalar(raw, raw, wmul[:, 0:1], 1.0, ALU.mult, ALU.min))
                link(dve.tensor_scalar(raw, raw, -1.0, ROUND, ALU.max, ALU.add))
                dve.tensor_scalar(wq[:, 2 * n:2 * n + 2, :].rearrange("p c d -> p (c d)"), raw,
                                  ROUND, None, ALU.subtract, saturate=False).then_inc(s_wq, 1)

            def assemble():
                for n in range(2):
                    dve.wait_ge(s_move[n], 16 * B * NG // 2)
                for n, dst in ((0, l1_wd[:, :, :, :].rearrange("p b k n -> p b (k n)")),
                               (1, l1_wu[:, :, :])):
                    slot = (2 * NG + n) % 4
                    dve.wait_ge(s_w[slot], 16 * (NG // 2) + 32)
                    for b in range(B):
                        link(dve.tensor_tensor(dst[:, b, :], dst[:, b, :],
                                               w_ring[:, slot, 512:1024], ALU.add))
                        dve.scalar_tensor_tensor(out=dst[:, b, :], in0=dst[:, b, :],
                                                 scalar=DELTA_SCALE, in1=w_ring[:, slot, 0:512],
                                                 op0=ALU.mult, op1=ALU.add).then_inc(s_l1w, 1)

            dve.memset(cond_sb[:, :], 0.0).then_inc(s_zero, 1)
            add_squares(0)
            u_max(0)
            u_max(1)
            condition()
            rsqrt(0)
            condition_scale()
            u_scale(0)
            prepare(0)
            u_low(0)
            u_scale(1)
            for p in range(STEPS):
                i, j = divmod(p, NP)
                if i == 0 and j + 1 < NP:
                    u_low(j + 1)
                    if j + 2 < NP:
                        u_max(j + 2)
                if i:
                    quantise(i - 1, j)
                multiply(p)
                if i == 0 and j + 2 < NP:
                    u_scale(j + 2)
                if j == STAT_PAIR - 2 and i + 1 < NB:
                    add_squares(i + 1)
                if j == STAT_PAIR + 1 and i + 1 < NB:
                    rsqrt(i + 1)
                if j % QG == QG - 1 and j < NP - 1:
                    group_max(i, j // QG)
                if i == 1 and j < 8:
                    down_quantise(j)
                if p == ASSEMBLE:
                    assemble()
                for n in range(NB):
                    if p == adapter_step(n) + 2:
                        for k in range(KD):
                            finish(n, k)
                if j == NP - 1:
                    if i + 1 < NB:
                        prepare(i + 1)
                    group_max(i, j // QG)
                    if i == 0:
                        down_mean()
                    if i > 0:
                        y_scale(i)
                        residual(i - 1, 0)
                    scales(i)
                    if i == 0:
                        down_scale()
                    else:
                        for k in range(1, KD):
                            residual(i - 1, k)
            i = NB - 1
            for c in range(NP):
                quantise(i, c)
                if c >= 4 and c % 2 == 0 and c // 2 - 2 < KD:
                    finish(i - 1, c // 2 - 2)
            y_scale(NB)
            for k in range(KD):
                residual(i, k)
            for k in range(KD):
                finish(i, k)


def kernel(x, cond_256, L0_cond_norm_w, L0_cond_up_w, L0_cond_down_w, L1_cond_Wd, L1_cond_bd,
           L1_cond_Wu, L1_cond_bu, L1_cond_Wdd, L1_cond_bdd, L1_cond_Wdu, L1_cond_bdu):
    import concourse.bacc as bacc
    from concourse.bass_utils import run_bass_kernel_spmd

    lay = {
        "x": np.asarray(x).reshape(NB, TB, KD, P).transpose(0, 3, 2, 1),
        "cond": np.asarray(cond_256).T,
        "norm_w": np.asarray(L0_cond_norm_w).T,
        "up_w": np.asarray(L0_cond_up_w).reshape(2, NP, P, KD, P).transpose(1, 4, 3, 0, 2)
            .reshape(NP, P, KD, UW),
        "down_w": np.asarray(L0_cond_down_w).reshape(D, NP // 2, 2, P).transpose(1, 3, 2, 0)
            .reshape(NP // 2, P, 2 * D),
        "Wd": np.asarray(L1_cond_Wd).reshape(BN, KD, P).transpose(2, 1, 0).reshape(P, KD * BN),
        "bd": np.asarray(L1_cond_bd).reshape(BN, 1),
        "Wu": np.asarray(L1_cond_Wu).T,
        "bu": np.asarray(L1_cond_bu).reshape(KD, P).T,
        "Wdd": np.asarray(L1_cond_Wdd).reshape(BN, KD, 4, NG_HALF, H).transpose(3, 4, 2, 1, 0)
            .reshape(NG_HALF, H, 2, 1024).transpose(0, 2, 1, 3).reshape(NG, H, 1024),
        "bdd": np.asarray(L1_cond_bdd).reshape(BN, KD, P).transpose(2, 1, 0).reshape(P, KD * BN),
        "Wdu": np.asarray(L1_cond_Wdu).reshape(D, 4, NG_HALF, H).transpose(2, 3, 1, 0)
            .reshape(NG_HALF, H, 2, 1024).transpose(0, 2, 1, 3).reshape(NG, H, 1024),
        "bdu": np.asarray(L1_cond_bdu).reshape(D, BN).T,
    }
    nc = bacc.Bacc("TRN2", target_bir_lowering=False, num_devices=1)
    arrays, args = {}, []
    for name, a in lay.items():
        a = np.ascontiguousarray(a)
        arrays[f"in_{name}"] = a
        args.append(nc.dram_tensor(f"in_{name}", a.shape, mybir.dt.from_np(a.dtype),
                                   kind="ExternalInput").ap())
    args.append(nc.dram_tensor("out", (NB, P, KD, TB), F32, kind="ExternalOutput").ap())
    build(nc, *args)
    got = run_bass_kernel_spmd(nc, [arrays], core_ids=[0]).results[0]["out"]
    return np.ascontiguousarray(got.transpose(0, 3, 2, 1)).reshape(B, S, D)
```

```python
from contextlib import ExitStack

import numpy as np

import concourse.bass as bass
from concourse import mybir
from concourse.alu_op_type import AluOpType as ALU

F32 = mybir.dt.float32
F16 = mybir.dt.float16
F8 = mybir.dt.float8e4
I32 = mybir.dt.int32
ACT = mybir.ActivationFunctionType
AX_X = mybir.AxisListType.X
AR = bass.bass_isa.ReduceOp

P = 128
B, S, D = 2, 2048, 512
FF = 2048
H = 128
BN = 128
TB = 512
WIDTHS = [TB] * (B * S // TB - 1) + [TB // 2] * 2
NB = len(WIDTHS)
FIRST = [sum(WIDTHS[:i]) for i in range(NB)]
BATCH = [t // S for t in FIRST]
LT = TB // 2
KD = D // P
NP = FF // P
UW = 2 * P
QG = 4

EPS_RMS = 1e-6
EPS_QUANT = 1e-5
DELTA_SCALE = 0.1
ROUND = 1.5 * 2.0 ** 23
EXP_MASK = 0x7F800000
RSQRT_SEED = 0x5F3759DF
NEWTON = 3
U_EXP, X_EXP = 14, 9

NG_HALF = BN * D // (4 * 512)
NG = 2 * NG_HALF

STEPS = NB * NP
DW_FIRST, DW_LAST = 4, 48
ASSEMBLE = DW_LAST + 1


def groups_of_step(p):
    n = DW_LAST - DW_FIRST + 1
    if not DW_FIRST <= p <= DW_LAST:
        return range(0)
    at = p - DW_FIRST
    return range(at * NG // n, (at + 1) * NG // n)


def adapter_step(i):
    return {0: 52, 1: 58}.get(i, (i + 2) * NP + 2)


def mid_free(n):
    return adapter_step(n) // NP - 1


STAT_PAIR = 10


def aux_plan():
    uses = [("stat", 0), ("scale", 0), ("rs", 0)]
    for p in range(STEPS):
        i, j = divmod(p, NP)
        uses += [("dw", g) for g in groups_of_step(p)]
        if j == STAT_PAIR and i + 1 < NB:
            uses.append(("stat", i + 1))
        for n in range(NB):
            if p == adapter_step(n):
                uses.append(("mid", n))
            if p == adapter_step(n) + 1:
                uses += [("up", n, k) for k in range(KD)]
        if j == NP - 2 and i + 1 < NB:
            uses.append(("rs", i + 1))
        if j == NP - 1:
            if i > 0:
                uses += [("y", i - 1, k) for k in range(KD)]
    uses += [("mid", NB - 2)] + [("up", NB - 2, k) for k in range(KD)]
    uses += [("y", NB - 1, k) for k in range(KD)]
    uses += [("mid", NB - 1)] + [("up", NB - 1, k) for k in range(KD)]
    return {key: n for n, key in enumerate(uses)}


def build(nc, x, cond, norm_w, up_w, down_w, Wd, bd, Wu, bu, Wdd, bdd, Wdu, bdu, out):
    aux = aux_plan()
    aux_keys = list(aux)
    with ExitStack() as ctx:
        def sb(name, shape, dt=F32):
            return ctx.enter_context(nc.sbuf_tensor(name, shape, dt))

        def sem(name):
            return ctx.enter_context(nc.semaphore(name))

        u_hi = sb("u_hi", [P, NP, KD, UW], F16)
        u_lo = sb("u_lo", [P, NP, KD, UW], F16)
        wq = sb("wq", [P, NP, D], F8)
        x_sb = sb("x_sb", [P, 4, KD, TB])
        x_hi = sb("x_hi", [P, KD, TB], F16)
        x_lo = sb("x_lo", [P, KD, TB], F16)
        h_sb = sb("h_sb", [P, NP, TB])
        q_sb = sb("q_sb", [P, NP, TB], F16)
        w_ring = sb("w_ring", [P, 4, 1024])
        gelu = sb("gelu", [P, 2, TB])
        tmp = sb("tmp", [P, 2, TB])
        work = sb("work", [P, TB])
        stage = sb("stage", [P, 2, TB])
        l1_wd = sb("l1_wd", [P, B, KD, BN])
        l1_wu = sb("l1_wu", [P, B, D])
        mid = sb("mid", [P, TB])
        hmax = sb("hmax", [P, TB])
        hstep = sb("hstep", [P, TB])
        qscale = sb("qscale", [P, TB])
        ident = sb("ident", [P, P])
        ones = sb("ones", [P, 1])
        cond_sb = sb("cond_sb", [P, 32])
        bd_sb = sb("bd_sb", [P, 1])
        bu_sb = sb("bu_sb", [P, KD])
        cs = sb("cs", [P, KD, B])
        cs_max = sb("cs_max", [P, B])
        cs_all = sb("cs_all", [P, B])
        cs_pow = sb("cs_pow", [P, B])
        cs_mul = sb("cs_mul", [P, B])
        cs_x = sb("cs_x", [P, KD, B])
        um = sb("um", [P, NP])
        um_all = sb("um_all", [P, NP])
        um_pow = sb("um_pow", [P, NP])
        um_mul = sb("um_mul", [P, NP])
        unscale = sb("unscale", [P, B, NP])
        dabs = sb("dabs", [P, 8])
        dsum = sb("dsum", [P, 1])
        dsum_all = sb("dsum_all", [P, 1])
        wmean = sb("wmean", [P, 1])
        wmul = sb("wmul", [P, 1])
        ms = sb("ms", [P, KD])
        ms_half = sb("ms_half", [P, KD])
        rs = sb("rs", [P, 2, KD])
        rs_t = sb("rs_t", [P, KD])
        u_raw = q_sb[:, :, :].rearrange("p c t -> p (c t)").bitcast(F32).rearrange(
            "p (s k m) -> p s k m", s=4, k=KD)
        d_raw = x_sb[:, 3, :, :].rearrange("p (s c) t -> p s (c t)", s=2)
        norm_raw = stage[:, 0, :]

        up_ps = [ctx.enter_context(nc.psum_tensor(f"up_ps{n}", [P, TB], F32)) for n in range(4)]
        aux_ps = [ctx.enter_context(nc.psum_tensor(f"aux_ps{n}", [P, TB], F32)) for n in range(4)]

        def bank(*key):
            return aux_ps[aux[key] % 4]

        s_small = sem("s_small")
        s_u = [sem(f"s_u{n}") for n in range(4)]
        s_d = [sem(f"s_d{n}") for n in range(2)]
        s_w = [sem(f"s_w{n}") for n in range(4)]
        s_x = [sem(f"s_load_x{n}") for n in range(4)]
        s_x0 = [sem(f"s_load_first{k}") for k in range(KD)]
        s_move = [sem(f"s_move{n}") for n in range(2)]
        s_store = [sem(f"s_store{n}") for n in range(4)]
        s_zero = sem("s_zero")
        s_const = sem("s_const")
        s_gate = sem("s_gate")
        s_val = sem("s_val")
        s_aux = sem("s_aux")
        s_um = sem("s_um")
        s_uma = sem("s_uma")
        s_umul = sem("s_umul")
        s_uhi = sem("s_uhi")
        s_ulo = sem("s_ulo")
        s_table = sem("s_table")
        s_cs = sem("s_cs")
        s_cm = sem("s_cm")
        s_cma = sem("s_cma")
        s_ms = sem("s_ms")
        s_sq = sem("s_sq")
        s_sqr = sem("s_sqr")
        s_rs = sem("s_rs")
        s_xs = sem("s_xs")
        s_xhi = sem("s_xhi")
        s_xlo = sem("s_xlo")
        s_gelu = sem("s_gelu")
        s_h = sem("s_h")
        s_gm = sem("s_gm")
        s_m = sem("s_m")
        s_ma = sem("s_ma")
        s_qm = sem("s_qm")
        s_q = sem("s_q")
        s_x1 = sem("s_x1")
        s_relu = sem("s_relu")
        s_out = sem("s_out")
        s_dabs = sem("s_dabs")
        s_dsum = sem("s_dsum")
        s_dsuma = sem("s_dsuma")
        s_wq = sem("s_wq")
        s_stage = sem("s_stage")
        s_l1w = sem("s_l1w")
        s_chain = sem("s_chain")

        def aux_ready(eng, *key):
            eng.wait_ge(s_aux, aux[key] + 1)

        def reader_done(key):
            kind, i = key[:2]
            return {
                "scale": (s_cs, 1),
                "stat": (s_ms, i + 1),
                "rs": (s_xs, KD * (i + 1)),
                "dw": (s_stage, i + 1),
                "y": (s_x1, KD * i + key[-1] + 1),
                "mid": (s_relu, i + 1),
                "up": (s_out, KD * i + key[-1] + 1),
            }[kind]

        block = ctx.enter_context(nc.Block())

        def pieces(i, dram, k=None):
            ks = slice(0, KD) if k is None else slice(k, k + 1)
            return [(x_sb[:, i % 4, ks, t:t + LT], dram[(FIRST[i] + t) // LT][:, ks, :])
                    for t in range(0, WIDTHS[i], LT)]

        def moved(i, first=0):
            return 16 * sum(WIDTHS[n] // LT for n in range(first, i + 1) if n % 4 == i % 4)

        @block.sync
        def _(sp):
            def load_u(j):
                if j >= 4:
                    sp.wait_ge(s_ulo, j - 3)
                sp.dma_start(u_raw[:, j % 4, :, :], up_w[j]).then_inc(s_u[j % 4], 16)

            def load_d(n):
                if 2 <= n < 10:
                    sp.wait_ge(s_dabs, n - 1)
                elif n >= 10:
                    sp.wait_ge(s_wq, n - 9)
                sp.dma_start(d_raw[:, n % 2, :], down_w[n % 8]).then_inc(s_d[n % 2], 16)

            def load_w(n):
                if n >= 4:
                    sp.wait_ge(s_aux, aux["dw", (n - 4) // 2] + 1)
                src = Wdd if n < NG else Wdu
                sp.dma_start(w_ring[:, n % 4, :], src[n % NG]).then_inc(s_w[n % 4], 16)

            def load_x(i):
                if i >= 4:
                    sp.wait_ge(s_store[i % 4], moved(i - 4))
                if i == 3:
                    sp.wait_ge(s_wq, 8)
                if i == 0:
                    for k in range(KD):
                        for dst, src in pieces(i, x, k):
                            sp.dma_start(dst, src).then_inc(s_x0[k], 16)
                    return
                for dst, src in pieces(i, x):
                    sp.dma_start(dst, src).then_inc(s_x[i % 4], 16)

            def store(i):
                sp.wait_ge(s_out, KD * (i + 1))
                for src, dst in pieces(i, out):
                    sp.dma_start(dst, src).then_inc(s_store[i % 4], 16)

            load_x(0)
            load_u(0)
            sp.dma_start(norm_raw, norm_w).then_inc(s_small, 16)
            sp.wait_ge(s_zero, 1)
            sp.dma_start(cond_sb[:, 0:B], cond).then_inc(s_small, 16)
            sp.dma_start(bd_sb[:, :], bd).then_inc(s_small, 16)
            sp.dma_start(bu_sb[:, :], bu).then_inc(s_small, 16)
            load_u(1)
            load_u(2)
            for g in groups_of_step(DW_FIRST):
                load_w(2 * g)
                load_w(2 * g + 1)
            for p in range(STEPS):
                i, j = divmod(p, NP)
                if i == 0 and j + 3 < NP:
                    load_u(j + 3)
                if i == 0 and j % 2 == 0:
                    load_d(j // 2)
                if i == 1 and j < 8:
                    load_d(8 + j)
                if p >= DW_FIRST:
                    for g in groups_of_step(p + 1):
                        load_w(2 * g)
                        load_w(2 * g + 1)
                if p == DW_LAST:
                    for n, parts in ((2 * NG, (Wd, bdd)), (2 * NG + 1, (Wu, bdu))):
                        sp.wait_ge(s_aux, aux["dw", (n - 4) // 2] + 1)
                        for c, part in enumerate(parts):
                            sp.dma_start(w_ring[:, n % 4, 512 * c:512 * c + 512], part)\
                                .then_inc(s_w[n % 4], 16)
                for n in range(NB):
                    if p == adapter_step(n) + 3:
                        store(n)
                        if n == 0:
                            load_x(4)
                if j == 4 and i + 1 < NB and i + 1 != 4:
                    load_x(i + 1)
            for i in (NB - 2, NB - 1):
                store(i)
            for n in range(4):
                sp.wait_ge(s_store[n], moved(max(range(n, NB, 4))))

        @block.gpsimd
        def _(pool):
            pool.memset(ones[:, :], 1.0).then_inc(s_const, 1)
            pool.memset(ident[:, :], 1.0).then_inc(s_const, 1)
            pool.wait_ge(s_const, 2)
            pool.affine_select(out=ident[:, :], in_=ident[:, :], compare_op=ALU.is_equal, fill=0.0,
                               base=0, pattern=[[-1, P]], channel_multiplier=1).then_inc(s_const, 1)

            def all_u(j):
                pool.wait_ge(s_um, j + 1)
                pool.partition_all_reduce(um_all[:, j:j + 1], um[:, j:j + 1], P, AR.absmax)\
                    .then_inc(s_uma, 1)

            def all_h(i):
                w = WIDTHS[i]
                pool.wait_ge(s_m, i + 1)
                pool.partition_all_reduce(work[:, 0:w], hmax[:, 0:w], P, AR.absmax)\
                    .then_inc(s_ma, 1)

            pool.wait_ge(s_cm, 1)
            pool.partition_all_reduce(cs_all[:, :], cs_max[:, :], P, AR.absmax).then_inc(s_cma, 1)
            for j in range(NP):
                all_u(j)
            all_h(0)
            pool.wait_ge(s_dsum, 1)
            pool.partition_all_reduce(dsum_all[:, :], dsum[:, :], P, AR.add).then_inc(s_dsuma, 1)
            for i in range(1, NB):
                all_h(i)

        @block.scalar
        def _(act):
            def squares(i):
                w = WIDTHS[i]
                if i:
                    act.wait_ge(s_x[i % 4], moved(i, 1))
                for k in range(KD):
                    if i == 0:
                        act.wait_ge(s_x0[k], moved(0))
                    n = (KD - 1) * i + k - 1
                    if k == 0:
                        if i:
                            act.wait_ge(s_gm, 2 * (i - 1) + 1)
                        dst = work[:, 0:w]
                    else:
                        if k <= 2 and i:
                            act.wait_ge(s_xlo, KD * i)
                        if k > 2:
                            act.wait_ge(s_sqr, n - 1)
                        dst = tmp[:, k % 2, 0:w]
                    act.activation(dst, x_sb[:, i % 4, k, 0:w], ACT.Square).then_inc(s_sq, 1)

            def x_high(i):
                w = WIDTHS[i]
                for k in range(KD):
                    act.wait_ge(s_xs, KD * i + k + 1)
                    act.activation(x_hi[:, k, 0:w], tmp[:, k % 2, 0:w], ACT.Copy)\
                        .then_inc(s_xhi, 1)

            def u_high(j):
                act.wait_ge(s_umul, 3 * j + 1)
                act.activation(u_hi[:, j, :, :], u_raw[:, j % 4, :, :], ACT.Copy,
                               scale=um_mul[:, j:j + 1]).then_inc(s_uhi, 1)

            def down_abs(n):
                act.wait_ge(s_d[n % 2], 16 * (n // 2 + 1))
                act.activation(d_raw[:, n % 2, :], d_raw[:, n % 2, :], ACT.Abs,
                               accum_out=dabs[:, n:n + 1]).then_inc(s_dabs, 1)

            def stage_group(g):
                aux_ready(act, "dw", g)
                if g >= 2:
                    act.wait_ge(s_move[g % 2], 16 * B * (g // 2))
                act.activation(stage[:, g % 2, :], bank("dw", g)[:, :], ACT.Copy)\
                    .then_inc(s_stage, 1)
                act.wait_ge(s_stage, g + 1)
                for b in range(B):
                    rows = stage[b:b + 97:32, g % 2, :]
                    if g < NG_HALF:
                        dst = l1_wd[g:g + 97:32, b, :, :].rearrange("q k n -> q (k n)")
                    else:
                        dst = l1_wu[g - NG_HALF:g - NG_HALF + 97:32, b, :]
                    act.dma_start(dst, rows).then_inc(s_move[g % 2], 16)

            def adapter_relu(n):
                aux_ready(act, "mid", n)
                if n:
                    aux_ready(act, "up", n - 1, KD - 1)
                w = WIDTHS[n]
                act.wait_ge(s_x1, KD * mid_free(n))
                act.activation(mid[:, 0:w], bank("mid", n)[:, 0:w], ACT.Relu, bias=bd_sb[:, 0:1])\
                    .then_inc(s_relu, 1)

            act.wait_ge(s_const, 1)
            act.activation(ms_half[:, 0:1], ones[:, :], ACT.Gelu).then_inc(s_table, 1)
            squares(0)
            u_high(0)
            x_high(0)
            u_high(1)
            for p in range(STEPS):
                i, j = divmod(p, NP)
                act.wait_ge(s_gate, p + 1)
                if i == 0:
                    act.wait_ge(s_umul, 3 * (j + 1))
                if p >= 2:
                    act.wait_ge(s_h, p - 1)
                w = WIDTHS[i]
                act.activation(gelu[:, p % 2, 0:w], up_ps[2 * (p % 2)][:, 0:w], ACT.Gelu,
                               scale=unscale[:, BATCH[i], j:j + 1]).then_inc(s_gelu, 1)
                if i == 0 and j + 2 < NP:
                    u_high(j + 2)
                if i == 0 and j % 2 == 1:
                    down_abs(j // 2)
                if j > 0:
                    for g in groups_of_step(p - 1):
                        stage_group(g)
                if j == STAT_PAIR - 2 and i + 1 < NB:
                    squares(i + 1)
                for n in range(NB):
                    if p == adapter_step(n) + 1:
                        adapter_relu(n)
                if j == NP - 1 and i + 1 < NB:
                    x_high(i + 1)
                if j == NP - 1:
                    for g in groups_of_step(p):
                        stage_group(g)
            adapter_relu(NB - 2)
            adapter_relu(NB - 1)

        @block.tensor
        def _(pe):
            def take(*key):
                n = aux[key]
                if n >= 4:
                    pe.wait_ge(*reader_done(aux_keys[n - 4]))
                return aux_ps[n % 4]

            def up_half(p, half, sem_):
                i, j = divmod(p, NP)
                ps = up_ps[2 * (p % 2) + (1 - half)]
                w = WIDTHS[i]
                cols = slice(P * half, P * half + P)
                for k in range(KD):
                    if j == 0 and half == 1:
                        pe.wait_ge(s_xhi, KD * i + k + 1)
                        pe.wait_ge(s_xlo, KD * i + k + 1)
                    whi, wlo = u_hi[:, j, k, cols], u_lo[:, j, k, cols]
                    xhi, xlo = x_hi[:, k, 0:w], x_lo[:, k, 0:w]
                    pe.matmul(ps[:, 0:w], whi, xhi, start=(k == 0), stop=False)
                    pe.matmul(ps[:, 0:w], whi, xlo, start=False, stop=False)
                    mm = pe.matmul(ps[:, 0:w], wlo, xhi, start=False, stop=(k == KD - 1))
                mm.then_inc(sem_, 1)

            def pair(p):
                if p < NP:
                    pe.wait_ge(s_uhi, p + 1)
                    pe.wait_ge(s_ulo, p + 1)
                if p >= 2:
                    pe.wait_ge(s_gelu, p - 1)
                up_half(p, 1, s_gate)
                if p >= 2:
                    pe.wait_ge(s_h, p - 1)
                up_half(p, 0, s_val)

            def adapter_group(g):
                ps = take("dw", g)
                for q in range(4):
                    n = 2 * g + q // 2
                    if q % 2 == 0:
                        pe.wait_ge(s_w[n % 4], 16 * (n // 4 + 1))
                    mm = pe.matmul(ps[32 * q:32 * q + 32, :], cond_sb[:, :],
                                   w_ring[:, n % 4, 512 * (q % 2):512 * (q % 2) + 512],
                                   start=True, stop=True)
                mm.then_inc(s_aux, 1)

            def stat(i):
                ps = take("stat", i)
                pe.wait_ge(s_sqr, (KD - 1) * (i + 1))
                for t in range(WIDTHS[i] // P):
                    mm = pe.matmul(ps[:, t:t + 1], work[:, P * t:P * t + P], ones[:, :],
                                   start=True, stop=True)
                mm.then_inc(s_aux, 1)

            def spread_rs(i):
                ps = take("rs", i)
                pe.wait_ge(s_rs, i + 1)
                for t in range(WIDTHS[i] // P):
                    mm = pe.transpose(ps[:, P * t:P * t + P],
                                      rs[:, i % 2, t:t + 1].to_broadcast([P, P]), ident[:, :])
                mm.then_inc(s_aux, 1)

            def down(i, k):
                ps = take("y", i, k)
                w = WIDTHS[i]
                if k == 0:
                    pe.wait_ge(s_q, NP * (i + 1))
                    pe.wait_ge(s_wq, 8)
                for c in range(NP):
                    mm = pe.matmul(ps[:, 0:w], wq[:, c, P * k:P * k + P], q_sb[:, c, 0:w],
                                   start=(c == 0), stop=(c == NP - 1))
                mm.then_inc(s_aux, 1)

            def last_down(i):
                w = WIDTHS[i]
                banks = [take("y", i, k) for k in range(KD)]
                for c in range(NP):
                    pe.wait_ge(s_q, NP * i + c + 1)
                    for k in range(KD):
                        mm = pe.matmul(banks[k][:, 0:w], wq[:, c, P * k:P * k + P],
                                       q_sb[:, c, 0:w],
                                       start=(c == 0), stop=(c == NP - 1))
                        if c == NP - 1:
                            mm.then_inc(s_aux, 1)

            def adapter_mid(i):
                ps = take("mid", i)
                w = WIDTHS[i]
                pe.wait_ge(s_l1w, 4)
                for k in range(KD):
                    pe.wait_ge(s_x1, KD * i + k + 1)
                    mm = pe.matmul(ps[:, 0:w], l1_wd[:, BATCH[i], k, :], x_sb[:, i % 4, k, 0:w],
                                   start=(k == 0), stop=(k == KD - 1))
                mm.then_inc(s_aux, 1)

            def adapter_up(i):
                pe.wait_ge(s_relu, i + 1)
                for k in range(KD):
                    ps = take("up", i, k)
                    w = WIDTHS[i]
                    pe.matmul(ps[:, 0:w], l1_wu[:, BATCH[i], P * k:P * k + P], mid[:, 0:w],
                              start=True, stop=True).then_inc(s_aux, 1)

            pe.wait_ge(s_const, 3)
            stat(0)
            pe.wait_ge(s_small, 64)
            ps = take("scale", 0)
            for k in range(KD):
                mm = pe.matmul(ps[:, B * k:B * k + B], norm_raw[:, P * k:P * k + P],
                               cond_sb[:, 0:B], start=True, stop=True)
            mm.then_inc(s_aux, 1)
            spread_rs(0)
            for p in range(STEPS):
                i, j = divmod(p, NP)
                pair(p)
                for g in groups_of_step(p):
                    adapter_group(g)
                if j == STAT_PAIR and i + 1 < NB:
                    stat(i + 1)
                for n in range(NB):
                    if p == adapter_step(n):
                        adapter_mid(n)
                    if p == adapter_step(n) + 1:
                        adapter_up(n)
                if j == NP - 2 and i + 1 < NB:
                    spread_rs(i + 1)
                if j == NP - 1:
                    if i > 0:
                        for k in range(KD):
                            down(i - 1, k)
            adapter_mid(NB - 2)
            adapter_up(NB - 2)
            last_down(NB - 1)
            adapter_mid(NB - 1)
            adapter_up(NB - 1)

        @block.vector
        def _(dve):
            links = [0]

            def link(ins):
                ins.then_inc(s_chain, 1)
                links[0] += 1
                dve.wait_ge(s_chain, links[0])

            def power_of_two(pow_, mul, top, exp, last):
                link(dve.tensor_scalar(mul, top, 1e-30, None, ALU.max))
                link(dve.tensor_scalar(pow_.bitcast(I32), mul.bitcast(I32), EXP_MASK, None,
                                       ALU.bitwise_and))
                ins = dve.tensor_scalar(mul.bitcast(I32), pow_.bitcast(I32), -1.0,
                                        float((254 + exp) * 2 ** 23), ALU.mult, ALU.add)
                last(ins)

            def u_max(j):
                dve.wait_ge(s_u[j % 4], 16 * (j // 4 + 1))
                dve.tensor_reduce(um[:, j:j + 1],
                                  u_raw[:, j % 4, :, :].rearrange("p k m -> p (k m)"), AX_X,
                                  ALU.max, apply_absolute_value=True).then_inc(s_um, 1)

            def u_scale(j):
                dve.wait_ge(s_uma, j + 1)
                power_of_two(um_pow[:, j:j + 1], um_mul[:, j:j + 1], um_all[:, j:j + 1], U_EXP,
                             lambda ins: ins.then_inc(s_umul, 1))
                for b in range(B):
                    dve.tensor_scalar(unscale[:, b, j:j + 1], um_pow[:, j:j + 1],
                                      2.0 ** -(U_EXP + X_EXP), cs_pow[:, b:b + 1],
                                      ALU.mult, ALU.mult).then_inc(s_umul, 1)

            def u_low(j):
                dve.wait_ge(s_uhi, j + 1)
                dve.wait_ge(s_umul, 3 * j + 1)
                flat = lambda t: t.rearrange("p k m -> p (k m)")
                dve.scalar_tensor_tensor(out=flat(u_lo[:, j, :, :]),
                                         in0=flat(u_raw[:, j % 4, :, :]),
                                         scalar=um_mul[:, j:j + 1], in1=flat(u_hi[:, j, :, :]),
                                         op0=ALU.mult, op1=ALU.subtract).then_inc(s_ulo, 1)

            def condition():
                aux_ready(dve, "scale", 0)
                ins = dve.tensor_scalar(cs[:, :, :].rearrange("p k b -> p (k b)"),
                                        bank("scale", 0)[:, 0:KD * B], 1.0, None, ALU.add)
                ins.then_inc(s_cs, 1)
                dve.wait_ge(s_cs, 1)
                dve.tensor_reduce(cs_max[:, :], cs[:, :, :].rearrange("p k b -> p b k"), AX_X,
                                  ALU.max, apply_absolute_value=True).then_inc(s_cm, 1)

            def condition_scale():
                dve.wait_ge(s_cma, 1)
                power_of_two(cs_pow[:, :], cs_mul[:, :], cs_all[:, :], X_EXP, link)
                for b in range(B):
                    link(dve.tensor_scalar(cs_x[:, :, b], cs[:, :, b], cs_mul[:, b:b + 1], None,
                                           ALU.mult))

            def add_squares(i):
                for k in range(1, KD):
                    dve.wait_ge(s_sq, KD * i + k + 1)
                    n = (KD - 1) * i + k
                    if k > 1:
                        dve.wait_ge(s_sqr, n - 1)
                    w = WIDTHS[i]
                    dve.tensor_tensor(work[:, 0:w], work[:, 0:w], tmp[:, k % 2, 0:w], ALU.add)\
                        .then_inc(s_sqr, 1)

            def rsqrt(i):
                aux_ready(dve, "stat", i)
                w = WIDTHS[i] // P
                ins = dve.tensor_scalar(ms[:, 0:w], bank("stat", i)[:, 0:w], 1.0 / D, EPS_RMS,
                                        ALU.mult, ALU.add)
                ins.then_inc(s_ms, 1)
                dve.wait_ge(s_ms, i + 1)
                if i == 0:
                    dve.wait_ge(s_table, 1)
                a, half, t, y = ms[:, 0:w], ms_half[:, 0:w], rs_t[:, 0:w], rs[:, i % 2, 0:w]
                link(dve.tensor_scalar(half, a, -0.5, None, ALU.mult))
                link(dve.tensor_scalar(t.bitcast(I32), a.bitcast(I32), 1, None,
                                       ALU.logical_shift_right))
                link(dve.tensor_scalar(y.bitcast(I32), t.bitcast(I32), -1.0, float(RSQRT_SEED),
                                       ALU.mult, ALU.add))
                for n in range(NEWTON):
                    link(dve.tensor_tensor(t, y, y, ALU.mult))
                    link(dve.tensor_tensor(t, t, half, ALU.mult))
                    ins = dve.scalar_tensor_tensor(out=y, in0=t, scalar=1.5, in1=y,
                                                   op0=ALU.add, op1=ALU.mult)
                    if n < NEWTON - 1:
                        link(ins)
                ins.then_inc(s_rs, 1)

            def prepare(i, aside=None):
                w = WIDTHS[i]
                aux_ready(dve, "rs", i)
                dve.wait_ge(s_sqr, (KD - 1) * (i + 1))
                if i:
                    dve.wait_ge(s_val, NP * i)

                def low(k):
                    dve.wait_ge(s_xhi, KD * i + k + 1)
                    dve.wait_ge(s_xs, KD * i + k + 1)
                    dve.tensor_tensor(x_lo[:, k, 0:w], tmp[:, k % 2, 0:w], x_hi[:, k, 0:w],
                                      ALU.subtract).then_inc(s_xlo, 1)

                for k in range(KD):
                    if k >= 2:
                        dve.wait_ge(s_xlo, KD * i + k - 1)
                    ins = dve.scalar_tensor_tensor(
                        out=tmp[:, k % 2, 0:w], in0=bank("rs", i)[:, 0:w],
                        scalar=cs_x[:, k, BATCH[i]:BATCH[i] + 1], in1=x_sb[:, i % 4, k, 0:w],
                        op0=ALU.mult, op1=ALU.mult)
                    ins.then_inc(s_xs, 1)
                    if k == 0 and aside:
                        aside()
                    if k >= 1:
                        low(k - 1)
                low(KD - 1)

            def multiply(p):
                i, j = divmod(p, NP)
                dve.wait_ge(s_val, p + 1)
                dve.wait_ge(s_gelu, p + 1)
                if i == 0:
                    dve.wait_ge(s_umul, 3 * (j + 1))
                else:
                    dve.wait_ge(s_q, p + 1 - NP)
                w = WIDTHS[i]
                dve.scalar_tensor_tensor(out=h_sb[:, j, 0:w], in0=up_ps[2 * (p % 2) + 1][:, 0:w],
                                         scalar=unscale[:, BATCH[i], j:j + 1],
                                         in1=gelu[:, p % 2, 0:w], op0=ALU.mult, op1=ALU.mult)\
                    .then_inc(s_h, 1)

            def group_max(i, g):
                c = QG * g
                dve.wait_ge(s_h, NP * i + c + QG)
                w = WIDTHS[i]
                src = h_sb[:, c:c + QG, 0:w].rearrange("p c t -> p t c")
                if g == 0:
                    if i:
                        dve.wait_ge(s_ma, i)
                    link(dve.tensor_reduce(hmax[:, 0:w], src, AX_X, ALU.max,
                                           apply_absolute_value=True))
                    return
                if g == 2 and i + 1 < NB:
                    aux_ready(dve, "stat", i + 1)
                link(dve.tensor_reduce(work[:, 0:w], src, AX_X, ALU.max, apply_absolute_value=True))
                ins = dve.tensor_tensor(hmax[:, 0:w], hmax[:, 0:w], work[:, 0:w], ALU.max)
                if g == NP // QG - 1:
                    ins.then_inc(s_m, 1)
                else:
                    ins.then_inc(s_gm, 1)
                    dve.wait_ge(s_gm, 2 * i + g)

            def scales(i):
                w = WIDTHS[i]
                dve.wait_ge(s_ma, i + 1)
                link(dve.tensor_scalar(hstep[:, 0:w], work[:, 0:w], EPS_QUANT, 1.0 / 127.0,
                                       ALU.max, ALU.mult))
                link(dve.reciprocal(qscale[:, 0:w], hstep[:, 0:w]))

            def y_scale(i):
                w = WIDTHS[i]
                if i >= 2:
                    aux_ready(dve, "up", i - 1, KD - 1)
                link(dve.tensor_scalar(mid[:, 0:w], hstep[:, 0:w], wmean[:, 0:1], None, ALU.mult))

            def q_product(i, c):
                w = WIDTHS[i]
                h = h_sb[:, c, 0:w]
                dve.tensor_tensor(h, h, qscale[:, 0:w], ALU.mult).then_inc(s_qm, 1)

            def q_round(i, c):
                w = WIDTHS[i]
                if c == 0 and i:
                    aux_ready(dve, "y", i - 1, KD - 1)
                dve.wait_ge(s_qm, NP * i + c + 1)
                dve.tensor_scalar(q_sb[:, c, 0:w], h_sb[:, c, 0:w], ROUND, -ROUND, ALU.add,
                                  ALU.add).then_inc(s_q, 1)

            def residual(i, k):
                aux_ready(dve, "y", i, k)
                w = WIDTHS[i]
                y, xk = bank("y", i, k)[:, 0:w], x_sb[:, i % 4, k, 0:w]
                link(dve.tensor_tensor(y, y, mid[:, 0:w], ALU.mult))
                dve.tensor_tensor(xk, y, xk, ALU.add).then_inc(s_x1, 1)

            def finish(i, k):
                aux_ready(dve, "up", i, k)
                w = WIDTHS[i]
                xk = x_sb[:, i % 4, k, 0:w]
                dve.scalar_tensor_tensor(out=xk, in0=bank("up", i, k)[:, 0:w],
                                         scalar=bu_sb[:, k:k + 1], in1=xk,
                                         op0=ALU.add, op1=ALU.add).then_inc(s_out, 1)

            def down_mean():
                dve.wait_ge(s_dabs, 8)
                dve.tensor_reduce(dsum[:, :], dabs[:, :], AX_X, ALU.add).then_inc(s_dsum, 1)

            def down_scale():
                dve.wait_ge(s_dsuma, 1)
                link(dve.tensor_scalar(wmean[:, :], dsum_all[:, :], 1.0 / (D * FF), 1e-5,
                                       ALU.mult, ALU.max))
                link(dve.reciprocal(wmul[:, :], wmean[:, :]))

            def down_quantise(n):
                dve.wait_ge(s_d[n % 2], 16 * (4 + n // 2 + 1))
                raw = d_raw[:, n % 2, :]
                link(dve.tensor_scalar(raw, raw, wmul[:, 0:1], 1.0, ALU.mult, ALU.min))
                link(dve.tensor_scalar(raw, raw, -1.0, ROUND, ALU.max, ALU.add))
                dve.tensor_scalar(wq[:, 2 * n:2 * n + 2, :].rearrange("p c d -> p (c d)"), raw,
                                  ROUND, None, ALU.subtract, saturate=False).then_inc(s_wq, 1)

            def assemble():
                for n in range(2):
                    dve.wait_ge(s_move[n], 16 * B * NG // 2)
                for n, dst in ((0, l1_wd[:, :, :, :].rearrange("p b k n -> p b (k n)")),
                               (1, l1_wu[:, :, :])):
                    slot = (2 * NG + n) % 4
                    dve.wait_ge(s_w[slot], 16 * (NG // 2) + 32)
                    for b in range(B):
                        link(dve.tensor_tensor(dst[:, b, :], dst[:, b, :],
                                               w_ring[:, slot, 512:1024], ALU.add))
                        dve.scalar_tensor_tensor(out=dst[:, b, :], in0=dst[:, b, :],
                                                 scalar=DELTA_SCALE, in1=w_ring[:, slot, 0:512],
                                                 op0=ALU.mult, op1=ALU.add).then_inc(s_l1w, 1)

            dve.memset(cond_sb[:, :], 0.0).then_inc(s_zero, 1)
            add_squares(0)
            u_max(0)
            condition()
            rsqrt(0)
            condition_scale()
            u_scale(0)
            u_max(1)
            prepare(0, lambda: u_low(0))
            u_scale(1)
            for p in range(STEPS):
                i, j = divmod(p, NP)
                if i == 0 and j + 1 < NP:
                    u_low(j + 1)
                    if j + 2 < NP:
                        u_max(j + 2)
                if i:
                    if j == 0:
                        q_product(i - 1, 0)
                    if j + 1 < NP:
                        q_product(i - 1, j + 1)
                    q_round(i - 1, j)
                multiply(p)
                if i == 0 and j + 2 < NP:
                    u_scale(j + 2)
                if j == STAT_PAIR - 2 and i + 1 < NB:
                    add_squares(i + 1)
                if j == STAT_PAIR + 1 and i + 1 < NB:
                    rsqrt(i + 1)
                if j % QG == QG - 1 and j < NP - 1:
                    group_max(i, j // QG)
                if i == 1 and j < 8:
                    down_quantise(j)
                if p == ASSEMBLE:
                    assemble()
                for n in range(NB):
                    if p == adapter_step(n) + 2:
                        for k in range(KD):
                            finish(n, k)
                if j == NP - 1:
                    if i + 1 < NB:
                        prepare(i + 1)
                    group_max(i, j // QG)
                    if i == 0:
                        down_mean()
                    if i > 0:
                        y_scale(i - 1)
                        residual(i - 1, 0)
                    scales(i)
                    if i == 0:
                        down_scale()
                    else:
                        for k in range(1, KD):
                            residual(i - 1, k)
            i = NB - 1
            q_product(i, 0)
            for c in range(NP):
                if c + 1 < NP:
                    q_product(i, c + 1)
                q_round(i, c)
                if 4 <= c < 4 + KD:
                    finish(i - 1, c - 4)
            y_scale(i)
            for k in range(KD):
                residual(i, k)
            for k in range(KD):
                finish(i, k)


def kernel(x, cond_256, L0_cond_norm_w, L0_cond_up_w, L0_cond_down_w, L1_cond_Wd, L1_cond_bd,
           L1_cond_Wu, L1_cond_bu, L1_cond_Wdd, L1_cond_bdd, L1_cond_Wdu, L1_cond_bdu):
    import concourse.bacc as bacc
    from concourse.bass_utils import run_bass_kernel_spmd

    lay = {
        "x": np.asarray(x).reshape(B * S // LT, LT, KD, P).transpose(0, 3, 2, 1),
        "cond": np.asarray(cond_256).T,
        "norm_w": np.asarray(L0_cond_norm_w).T,
        "up_w": np.asarray(L0_cond_up_w).reshape(2, NP, P, KD, P).transpose(1, 4, 3, 0, 2)
            .reshape(NP, P, KD, UW),
        "down_w": np.asarray(L0_cond_down_w).reshape(D, NP // 2, 2, P).transpose(1, 3, 2, 0)
            .reshape(NP // 2, P, 2 * D),
        "Wd": np.asarray(L1_cond_Wd).reshape(BN, KD, P).transpose(2, 1, 0).reshape(P, KD * BN),
        "bd": np.asarray(L1_cond_bd).reshape(BN, 1),
        "Wu": np.asarray(L1_cond_Wu).T,
        "bu": np.asarray(L1_cond_bu).reshape(KD, P).T,
        "Wdd": np.asarray(L1_cond_Wdd).reshape(BN, KD, 4, NG_HALF, H).transpose(3, 4, 2, 1, 0)
            .reshape(NG_HALF, H, 2, 1024).transpose(0, 2, 1, 3).reshape(NG, H, 1024),
        "bdd": np.asarray(L1_cond_bdd).reshape(BN, KD, P).transpose(2, 1, 0).reshape(P, KD * BN),
        "Wdu": np.asarray(L1_cond_Wdu).reshape(D, 4, NG_HALF, H).transpose(2, 3, 1, 0)
            .reshape(NG_HALF, H, 2, 1024).transpose(0, 2, 1, 3).reshape(NG, H, 1024),
        "bdu": np.asarray(L1_cond_bdu).reshape(D, BN).T,
    }
    nc = bacc.Bacc("TRN2", target_bir_lowering=False, num_devices=1)
    arrays, args = {}, []
    for name, a in lay.items():
        a = np.ascontiguousarray(a)
        arrays[f"in_{name}"] = a
        args.append(nc.dram_tensor(f"in_{name}", a.shape, mybir.dt.from_np(a.dtype),
                                   kind="ExternalInput").ap())
    args.append(nc.dram_tensor("out", (B * S // LT, P, KD, LT), F32, kind="ExternalOutput").ap())
    build(nc, *args)
    got = run_bass_kernel_spmd(nc, [arrays], core_ids=[0]).results[0]["out"]
    return np.ascontiguousarray(got.transpose(0, 3, 2, 1)).reshape(B, S, D)
```

```python
from contextlib import ExitStack

import numpy as np

import concourse.bass as bass
from concourse import mybir
from concourse.alu_op_type import AluOpType as ALU

F32 = mybir.dt.float32
F16 = mybir.dt.float16
F8 = mybir.dt.float8e4
I32 = mybir.dt.int32
ACT = mybir.ActivationFunctionType
AX_X = mybir.AxisListType.X
AR = bass.bass_isa.ReduceOp

P = 128
B, S, D = 2, 2048, 512
FF = 2048
H = 128
BN = 128
TB = 512
NT = TB // P
NB = B * S // TB
BATCH = [i * TB // S for i in range(NB)]
KD = D // P
NP = FF // P
UW = 2 * P
QG = 4

EPS_RMS = 1e-6
EPS_QUANT = 1e-5
DELTA_SCALE = 0.1
ROUND = 1.5 * 2.0 ** 23
EXP_MASK = 0x7F800000
RSQRT_SEED = 0x5F3759DF
NEWTON = 3
U_EXP, X_EXP = 14, 9

NG_HALF = BN * D // (4 * 512)
NG = 2 * NG_HALF

STEPS = NB * NP
EARLY = 2
DW_FIRST, DW_LAST = 4, 79
ASSEMBLE = DW_LAST + 1


def groups_of_step(p):
    if not DW_FIRST <= p <= DW_LAST:
        return range(0)

    def before(q):
        q -= q % NP == NP - 1
        return EARLY + max(q - DW_FIRST, 0) * (NG - EARLY) // (DW_LAST + 1 - DW_FIRST)

    return range(before(p), before(p + 1))


PARKED = (0, 1, 2)
ADAPTER_STEP = {3: ASSEMBLE + 2, 0: 5 * NP + 9, 4: 6 * NP + 2, 5: 7 * NP + 2}
BACK_STEP = {0: 5 * NP + 6, 2: 6 * NP + 6, 1: 7 * NP + 6}
TAIL = (2, 6), (1, 7)
ADAPTERS = list(ADAPTER_STEP) + list(TAIL[0] + TAIL[1])
TENANTS = [[("x", 0), ("x", 4), ("back", 2)],
           [("x", 1), ("x", 5), ("back", 1)],
           [("x", 2), ("x", 6)],
           [("x", 3), ("back", 0), ("x", 7)]]
FIRST_IN = [1, 0, 0, 0]


def seat(kind, i):
    return next((slot, t.index((kind, i))) for slot, t in enumerate(TENANTS) if (kind, i) in t)


SQUARES = 8
GROUP_MAX = (3, 7, 14)
STAT_PAIR = 12


def aux_plan():
    def adapter(n):
        return [("mid", n)] + [("up", n, k) for k in range(KD)]

    uses = [("scale", 0), ("stat", 0), ("dw", 0), ("rs", 0), ("dw", 1)]
    for p in range(STEPS):
        i, j = divmod(p, NP)
        uses += [("dw", g) for g in groups_of_step(p)]
        if j == STAT_PAIR and i + 1 < NB:
            uses.append(("stat", i + 1))
        for n, step in ADAPTER_STEP.items():
            if p == step:
                uses += adapter(n)
        if j == NP - 2 and i + 1 < NB:
            uses.append(("rs", i + 1))
        if j == NP - 1 and i > 0:
            uses += [("y", i - 1, k) for k in range(KD)]
    for two in TAIL:
        uses += [("mid", n) for n in two] + [("up", n, k) for n in two for k in range(KD)]
    return {key: n for n, key in enumerate(uses)}


def build(nc, x, cond, norm_w, up_w, down_w, Wd, bd, Wu, bu, Wdd, bdd, Wdu, bdu, out):
    aux = aux_plan()
    aux_keys = list(aux)
    with ExitStack() as ctx:
        def sb(name, shape, dt=F32):
            return ctx.enter_context(nc.sbuf_tensor(name, shape, dt))

        def sem(name):
            return ctx.enter_context(nc.semaphore(name))

        u_hi = sb("u_hi", [P, NP, KD, UW], F16)
        u_lo = sb("u_lo", [P, NP, KD, UW], F16)
        wq = sb("wq", [P, NP, D], F8)
        x_sb = sb("x_sb", [P, 4, KD, TB])
        x_hi = sb("x_hi", [P, KD, TB], F16)
        x_lo = sb("x_lo", [P, KD, TB], F16)
        h_sb = sb("h_sb", [P, NP, TB])
        q_sb = sb("q_sb", [P, NP, TB], F16)
        w_ring = sb("w_ring", [P, 4, 1024])
        gelu = sb("gelu", [P, 2, TB])
        tmp = sb("tmp", [P, 2, TB])
        work = sb("work", [P, TB])
        stage = sb("stage", [P, 2, TB])
        l1_wd = sb("l1_wd", [P, B, KD, BN])
        l1_wu = sb("l1_wu", [P, B, D])
        yscale = sb("yscale", [P, TB])
        hmax = sb("hmax", [P, TB])
        hstep = sb("hstep", [P, TB])
        qscale = sb("qscale", [P, TB])
        ident = sb("ident", [P, P])
        ones = sb("ones", [P, 1])
        cond_sb = sb("cond_sb", [P, 32])
        bd_sb = sb("bd_sb", [P, 1])
        bu_sb = sb("bu_sb", [P, KD])
        cs = sb("cs", [P, KD, B])
        cs_max = sb("cs_max", [P, B])
        cs_all = sb("cs_all", [P, B])
        cs_pow = sb("cs_pow", [P, B])
        cs_mul = sb("cs_mul", [P, B])
        cs_x = sb("cs_x", [P, KD, B])
        um = sb("um", [P, NP])
        um_all = sb("um_all", [P, NP])
        um_pow = sb("um_pow", [P, NP])
        um_mul = sb("um_mul", [P, NP])
        unscale = sb("unscale", [P, B, NP])
        dabs = sb("dabs", [P, 8])
        dsum = sb("dsum", [P, 1])
        dsum_all = sb("dsum_all", [P, 1])
        wmean = sb("wmean", [P, 1])
        wmul = sb("wmul", [P, 1])
        ms = sb("ms", [P, NT])
        ms_half = sb("ms_half", [P, NT])
        rs = sb("rs", [P, 2, NT])
        rs_t = sb("rs_t", [P, NT])
        u_raw = q_sb[:, :, :].rearrange("p c t -> p (c t)").bitcast(F32).rearrange(
            "p (s k m) -> p s k m", s=4, k=KD)
        d_raw = x_sb[:, 3, :, :].rearrange("p (s c) t -> p s (c t)", s=2)
        norm_raw = stage[:, 0, :]

        up_ps = [ctx.enter_context(nc.psum_tensor(f"up_ps{n}", [P, TB], F32)) for n in range(4)]
        aux_ps = [ctx.enter_context(nc.psum_tensor(f"aux_ps{n}", [P, TB], F32)) for n in range(4)]

        def bank(*key):
            return aux_ps[aux[key] % 4]

        s_small = sem("s_small")
        s_u = [sem(f"s_u{n}") for n in range(4)]
        s_d = [sem(f"s_d{n}") for n in range(2)]
        s_w = [sem(f"s_w{n}") for n in range(4)]
        s_x = [sem(f"s_load_x{n}") for n in range(4)]
        s_x0 = [sem(f"s_load_first{k}") for k in range(KD)]
        s_move = [sem(f"s_move{n}") for n in range(2)]
        s_store = [sem(f"s_store{n}") for n in range(4)]
        s_last_store = sem("s_last_store")
        s_zero = sem("s_zero")
        s_const = sem("s_const")
        s_gate = sem("s_gate")
        s_val = sem("s_val")
        s_aux = sem("s_aux")
        s_last = sem("s_last")
        s_um = sem("s_um")
        s_uma = sem("s_uma")
        s_umul = sem("s_umul")
        s_uhi = sem("s_uhi")
        s_ulo = sem("s_ulo")
        s_table = sem("s_table")
        s_cs = sem("s_cs")
        s_cm = sem("s_cm")
        s_cma = sem("s_cma")
        s_ms = sem("s_ms")
        s_sq = sem("s_sq")
        s_sqr = sem("s_sqr")
        s_rs = sem("s_rs")
        s_xs = sem("s_xs")
        s_xhi = sem("s_xhi")
        s_xlo = sem("s_xlo")
        s_gelu = sem("s_gelu")
        s_h = sem("s_h")
        s_gm = sem("s_gm")
        s_m = sem("s_m")
        s_ma = sem("s_ma")
        s_qm = sem("s_qm")
        s_q = sem("s_q")
        s_y = sem("s_y")
        s_x1 = sem("s_x1")
        s_relu = sem("s_relu")
        s_out = sem("s_out")
        s_dabs = sem("s_dabs")
        s_dsum = sem("s_dsum")
        s_dsuma = sem("s_dsuma")
        s_wq = sem("s_wq")
        s_stage = sem("s_stage")
        s_l1w = sem("s_l1w")
        s_chain = sem("s_chain")

        def aux_ready(eng, *key):
            eng.wait_ge(s_aux, aux[key] + 1)

        def reader_done(key):
            kind, i = key[:2]

            def position(n):
                return ADAPTERS.index(n) if n in ADAPTERS else 0

            return {
                "scale": (s_cs, 1),
                "stat": (s_ms, i + 1),
                "rs": (s_xs, KD * (i + 1)),
                "dw": (s_stage, i + 1),
                "y": (s_x1, KD * i + key[-1] + 1),
                "mid": (s_relu, position(i) + 1),
                "up": (s_out, KD * position(i) + key[-1] + 1),
            }[kind]

        block = ctx.enter_context(nc.Block())

        def arrived(kind, i):
            slot, n = seat(kind, i)
            return s_x[slot], 16 * (n + 1 - FIRST_IN[slot])

        def left(kind, i):
            slot, n = seat(kind, i)
            return s_store[slot], 16 * (n + 1)

        def on_chip(kind, i):
            return x_sb[:, seat(kind, i)[0], :, :]

        def in_dram(dram, i):
            return dram[:, :, TB * i:TB * i + TB]

        @block.sync
        def _(sp):
            def load_u(j):
                if j >= 4:
                    sp.wait_ge(s_ulo, j - 3)
                sp.dma_start(u_raw[:, j % 4, :, :], up_w[j]).then_inc(s_u[j % 4], 16)

            def load_d(n):
                if 2 <= n < 10:
                    sp.wait_ge(s_dabs, n - 1)
                elif n >= 10:
                    sp.wait_ge(s_wq, n - 9)
                sp.dma_start(d_raw[:, n % 2, :], down_w[n % 8]).then_inc(s_d[n % 2], 16)

            def load_w(n):
                if n >= 4:
                    sp.wait_ge(s_aux, aux["dw", (n - 4) // 2] + 1)
                src = Wdd if n < NG else Wdu
                sp.dma_start(w_ring[:, n % 4, :], src[n % NG]).then_inc(s_w[n % 4], 16)

            def load(kind, i):
                slot, n = seat(kind, i)
                if n:
                    sp.wait_ge(*left(*TENANTS[slot][n - 1]))
                if (kind, i) == ("x", 3):
                    sp.wait_ge(s_wq, 8)
                if kind == "back":
                    sp.wait_ge(*left("x", i))
                    sp.dma_start(on_chip(kind, i), in_dram(out, i)).then_inc(s_x[slot], 16)
                else:
                    sp.dma_start(on_chip(kind, i), in_dram(x, i)).then_inc(s_x[slot], 16)

            def load_first():
                for k in range(KD):
                    sp.dma_start(on_chip("x", 0)[:, k, :], in_dram(x, 0)[:, k, :])\
                        .then_inc(s_x0[k], 16)

            def park(i):
                sp.wait_ge(s_x1, KD * (i + 1))
                sp.dma_start(in_dram(out, i), on_chip("x", i)).then_inc(left("x", i)[0], 16)

            def store(i):
                tenant = ("back" if i in PARKED else "x", i)
                sp.wait_ge(s_out, KD * (ADAPTERS.index(i) + 1))
                sp.dma_start(in_dram(out, i), on_chip(*tenant)).then_inc(left(*tenant)[0], 16)

            load_first()
            sp.dma_start(norm_raw, norm_w).then_inc(s_small, 16)
            sp.wait_ge(s_zero, 1)
            sp.dma_start(cond_sb[:, 0:B], cond).then_inc(s_small, 16)
            sp.dma_start(bd_sb[:, :], bd).then_inc(s_small, 16)
            sp.dma_start(bu_sb[:, :], bu).then_inc(s_small, 16)
            load_u(0)
            for n in range(2 * EARLY):
                load_w(n)
                if n == 1:
                    load_u(1)
            load_u(2)
            for g in groups_of_step(DW_FIRST):
                load_w(2 * g)
                load_w(2 * g + 1)
            for p in range(STEPS):
                i, j = divmod(p, NP)
                if i == 0 and j + 3 < NP:
                    load_u(j + 3)
                if i == 0 and j % 2 == 0:
                    load_d(j // 2)
                if i == 1 and j < 8:
                    load_d(8 + j)
                if p >= DW_FIRST:
                    for g in groups_of_step(p + 1):
                        load_w(2 * g)
                        load_w(2 * g + 1)
                if p == DW_LAST:
                    for n, parts in ((2 * NG, (Wd, bdd)), (2 * NG + 1, (Wu, bdu))):
                        sp.wait_ge(s_aux, aux["dw", (n - 4) // 2] + 1)
                        for c, part in enumerate(parts):
                            sp.dma_start(w_ring[:, n % 4, 512 * c:512 * c + 512], part)\
                                .then_inc(s_w[n % 4], 16)
                if j == 2 and i - 2 in PARKED:
                    park(i - 2)
                if j == 4 and i + 1 < NB:
                    load("x", i + 1)
                for n in ADAPTERS:
                    if p == ADAPTER_STEP.get(n, STEPS) + 3:
                        store(n)
                    if p == BACK_STEP.get(n):
                        load("back", n)
            for n in TAIL[0]:
                store(n)
            for a, tenant in ((NB - 2, ("back", TAIL[1][0])), (NB - 1, ("x", TAIL[1][1]))):
                for k in range(KD):
                    sp.wait_ge(s_out, KD * a + k + 1)
                    sp.dma_start(in_dram(out, tenant[1])[:, k, :], on_chip(*tenant)[:, k, :])\
                        .then_inc(s_last_store, 16)
            sp.wait_ge(s_last_store, 16 * 2 * KD)
            for n in ADAPTERS[:-2]:
                sp.wait_ge(*left("back" if n in PARKED else "x", n))

        @block.gpsimd
        def _(pool):
            pool.memset(ones[:, :], 1.0).then_inc(s_const, 1)
            pool.memset(ident[:, :], 1.0).then_inc(s_const, 1)
            pool.wait_ge(s_const, 2)
            pool.affine_select(out=ident[:, :], in_=ident[:, :], compare_op=ALU.is_equal, fill=0.0,
                               base=0, pattern=[[-1, P]], channel_multiplier=1).then_inc(s_const, 1)

            def all_u(j):
                pool.wait_ge(s_um, j + 1)
                pool.partition_all_reduce(um_all[:, j:j + 1], um[:, j:j + 1], P, AR.absmax)\
                    .then_inc(s_uma, 1)

            def all_h(i):
                pool.wait_ge(s_m, i + 1)
                pool.partition_all_reduce(work[:, :], hmax[:, :], P, AR.absmax)\
                    .then_inc(s_ma, 1)

            pool.wait_ge(s_cm, 1)
            pool.partition_all_reduce(cs_all[:, :], cs_max[:, :], P, AR.absmax).then_inc(s_cma, 1)
            for j in range(NP):
                all_u(j)
            pool.wait_ge(s_dsum, 1)
            pool.partition_all_reduce(dsum_all[:, :], dsum[:, :], P, AR.add).then_inc(s_dsuma, 1)
            for i in range(NB):
                all_h(i)

        @block.scalar
        def _(act):
            def squares(i, ks):
                for k in ks:
                    if i == 0:
                        act.wait_ge(s_x0[k], 16)
                    elif k == 0:
                        act.wait_ge(*arrived("x", i))
                    n = (KD - 1) * i + k - 1
                    if k == 0:
                        if i:
                            act.wait_ge(s_gm, 2 * (i - 1) + 1)
                        dst = work[:, :]
                    else:
                        if k <= 2 and i:
                            act.wait_ge(s_xlo, KD * i)
                        if k > 2:
                            act.wait_ge(s_sqr, n - 1)
                        dst = tmp[:, k % 2, :]
                    act.activation(dst, x_sb[:, i % 4, k, :], ACT.Square).then_inc(s_sq, 1)

            def x_high(i):
                if i:
                    act.wait_ge(s_val, NP * i)
                for k in range(KD):
                    act.wait_ge(s_xs, KD * i + k + 1)
                    act.activation(x_hi[:, k, :], tmp[:, k % 2, :], ACT.Copy)\
                        .then_inc(s_xhi, 1)

            def u_high(j):
                act.wait_ge(s_umul, 3 * j + 1)
                act.activation(u_hi[:, j, :, :], u_raw[:, j % 4, :, :], ACT.Copy,
                               scale=um_mul[:, j:j + 1]).then_inc(s_uhi, 1)

            def down_abs(n):
                act.wait_ge(s_d[n % 2], 16 * (n // 2 + 1))
                act.activation(d_raw[:, n % 2, :], d_raw[:, n % 2, :], ACT.Abs,
                               accum_out=dabs[:, n:n + 1]).then_inc(s_dabs, 1)

            def stage_group(g):
                aux_ready(act, "dw", g)
                if g >= 2:
                    act.wait_ge(s_move[g % 2], 16 * B * (g // 2))
                act.activation(stage[:, g % 2, :], bank("dw", g)[:, :], ACT.Copy)\
                    .then_inc(s_stage, 1)
                act.wait_ge(s_stage, g + 1)
                for b in range(B):
                    rows = stage[b:b + 97:32, g % 2, :]
                    if g < NG_HALF:
                        dst = l1_wd[g:g + 97:32, b, :, :].rearrange("q k n -> q (k n)")
                    else:
                        dst = l1_wu[g - NG_HALF:g - NG_HALF + 97:32, b, :]
                    act.dma_start(dst, rows).then_inc(s_move[g % 2], 16)

            def adapter_relu(n):
                a = ADAPTERS.index(n)
                aux_ready(act, "mid", n)
                if a >= 2:
                    aux_ready(act, "up", ADAPTERS[a - 2], KD - 1)
                act.activation(stage[:, a % 2, :], bank("mid", n)[:, :], ACT.Relu,
                               bias=bd_sb[:, 0:1]).then_inc(s_relu, 1)

            act.wait_ge(s_const, 1)
            act.activation(ms_half[:, 0:1], ones[:, :], ACT.Gelu).then_inc(s_table, 1)
            squares(0, range(KD))
            u_high(0)
            x_high(0)
            u_high(1)
            for g in range(EARLY):
                stage_group(g)
            for p in range(STEPS):
                i, j = divmod(p, NP)
                act.wait_ge(s_gate, p + 1)
                if i == 0:
                    act.wait_ge(s_umul, 3 * (j + 1))
                if p >= 2:
                    act.wait_ge(s_h, p - 1)
                act.activation(gelu[:, p % 2, :], up_ps[2 * (p % 2)][:, :], ACT.Gelu,
                               scale=unscale[:, BATCH[i], j:j + 1]).then_inc(s_gelu, 1)
                if i == 0 and j + 2 < NP:
                    u_high(j + 2)
                if i == 0 and j % 2 == 1:
                    down_abs(j // 2)
                if j > 0:
                    for g in groups_of_step(p - 1):
                        stage_group(g)
                if 0 <= j - SQUARES < KD - 1 and i + 1 < NB:
                    squares(i + 1, range(2) if j == SQUARES else (j - SQUARES + 1,))
                for n, step in ADAPTER_STEP.items():
                    if p == step + 1:
                        adapter_relu(n)
                if j == NP - 1 and i + 1 < NB:
                    x_high(i + 1)
                if j == NP - 1:
                    for g in groups_of_step(p):
                        stage_group(g)
            for n in ADAPTERS[-4:]:
                adapter_relu(n)

        @block.tensor
        def _(pe):
            def take(*key):
                n = aux[key]
                if n >= 4:
                    pe.wait_ge(*reader_done(aux_keys[n - 4]))
                return aux_ps[n % 4]

            def up_chunk(p, half, k):
                i, j = divmod(p, NP)
                ps = up_ps[2 * (p % 2) + (1 - half)][:, :]
                cols = slice(P * half, P * half + P)
                whi, wlo = u_hi[:, j, k, cols], u_lo[:, j, k, cols]
                xhi, xlo = x_hi[:, k, :], x_lo[:, k, :]
                pe.matmul(ps, whi, xhi, start=(k == 0), stop=False)
                pe.matmul(ps, whi, xlo, start=False, stop=False)
                mm = pe.matmul(ps, wlo, xhi, start=False, stop=(k == KD - 1))
                if k == KD - 1:
                    mm.then_inc(s_gate if half else s_val, 1)

            def pair(p):
                i, j = divmod(p, NP)
                if i == 0:
                    pe.wait_ge(s_uhi, p + 1)
                    pe.wait_ge(s_ulo, p + 1)
                if p >= 2:
                    pe.wait_ge(s_gelu, p - 1)
                if j == 0:
                    if p >= 2:
                        pe.wait_ge(s_h, p - 1)
                    for k in range(KD):
                        pe.wait_ge(s_xhi, KD * i + k + 1)
                        pe.wait_ge(s_xlo, KD * i + k + 1)
                        up_chunk(p, 1, k)
                        up_chunk(p, 0, k)
                    return
                for k in range(KD):
                    up_chunk(p, 1, k)
                if p >= 2:
                    pe.wait_ge(s_h, p - 1)
                for k in range(KD):
                    up_chunk(p, 0, k)

            def adapter_group(g):
                ps = take("dw", g)
                for q in range(4):
                    n = 2 * g + q // 2
                    if q % 2 == 0:
                        pe.wait_ge(s_w[n % 4], 16 * (n // 4 + 1))
                    mm = pe.matmul(ps[32 * q:32 * q + 32, :], cond_sb[:, :],
                                   w_ring[:, n % 4, 512 * (q % 2):512 * (q % 2) + 512],
                                   start=True, stop=True)
                mm.then_inc(s_aux, 1)

            def stat(i):
                ps = take("stat", i)
                pe.wait_ge(s_sqr, (KD - 1) * (i + 1))
                for t in range(NT):
                    mm = pe.matmul(ps[:, t:t + 1], work[:, P * t:P * t + P], ones[:, :],
                                   start=True, stop=True)
                mm.then_inc(s_aux, 1)

            def spread_rs(i):
                ps = take("rs", i)
                pe.wait_ge(s_rs, i + 1)
                for t in range(NT):
                    mm = pe.transpose(ps[:, P * t:P * t + P],
                                      rs[:, i % 2, t:t + 1].to_broadcast([P, P]), ident[:, :])
                mm.then_inc(s_aux, 1)

            def down(i, k):
                ps = take("y", i, k)
                if k == 0:
                    pe.wait_ge(s_q, NP * (i + 1))
                    pe.wait_ge(s_wq, 8)
                for c in range(NP):
                    mm = pe.matmul(ps[:, :], wq[:, c, P * k:P * k + P], q_sb[:, c, :],
                                   start=(c == 0), stop=(c == NP - 1))
                mm.then_inc(s_aux, 1)

            def last_down(i):
                banks = up_ps
                for c in range(NP):
                    pe.wait_ge(s_q, NP * i + c + 1)
                    for k in range(KD):
                        mm = pe.matmul(banks[k][:, :], wq[:, c, P * k:P * k + P],
                                       q_sb[:, c, :],
                                       start=(c == 0), stop=(c == NP - 1))
                        if c == NP - 1:
                            mm.then_inc(s_last, 1)

            def adapter_mid(i):
                kind = "back" if i in PARKED else "x"
                ps = take("mid", i)
                pe.wait_ge(s_l1w, 4)
                if kind == "back":
                    pe.wait_ge(*arrived(kind, i))
                for k in range(KD):
                    if kind == "x":
                        pe.wait_ge(s_x1, KD * i + k + 1)
                    mm = pe.matmul(ps[:, :], l1_wd[:, BATCH[i], k, :], on_chip(kind, i)[:, k, :],
                                   start=(k == 0), stop=(k == KD - 1))
                mm.then_inc(s_aux, 1)

            def adapter_up(i):
                a = ADAPTERS.index(i)
                pe.wait_ge(s_relu, a + 1)
                for k in range(KD):
                    ps = take("up", i, k)
                    pe.matmul(ps[:, :], l1_wu[:, BATCH[i], P * k:P * k + P], stage[:, a % 2, :],
                              start=True, stop=True).then_inc(s_aux, 1)

            pe.wait_ge(s_const, 3)
            pe.wait_ge(s_small, 64)
            ps = take("scale", 0)
            for k in range(KD):
                mm = pe.matmul(ps[:, B * k:B * k + B], norm_raw[:, P * k:P * k + P],
                               cond_sb[:, 0:B], start=True, stop=True)
            mm.then_inc(s_aux, 1)
            stat(0)
            adapter_group(0)
            spread_rs(0)
            adapter_group(1)
            for p in range(STEPS):
                i, j = divmod(p, NP)
                pair(p)
                for g in groups_of_step(p):
                    adapter_group(g)
                if j == STAT_PAIR and i + 1 < NB:
                    stat(i + 1)
                for n, step in ADAPTER_STEP.items():
                    if p == step:
                        adapter_mid(n)
                    if p == step + 1:
                        adapter_up(n)
                if j == NP - 2 and i + 1 < NB:
                    spread_rs(i + 1)
                if j == NP - 1:
                    if i > 0:
                        for k in range(KD):
                            down(i - 1, k)
            for two in TAIL:
                if two == TAIL[-1]:
                    last_down(NB - 1)
                for n in two:
                    adapter_mid(n)
                for n in two:
                    adapter_up(n)

        @block.vector
        def _(dve):
            links = [0]

            def link(ins):
                ins.then_inc(s_chain, 1)
                links[0] += 1
                dve.wait_ge(s_chain, links[0])

            def power_of_two(pow_, mul, top, exp, last):
                link(dve.tensor_scalar(mul, top, 1e-30, None, ALU.max))
                link(dve.tensor_scalar(pow_.bitcast(I32), mul.bitcast(I32), EXP_MASK, None,
                                       ALU.bitwise_and))
                ins = dve.tensor_scalar(mul.bitcast(I32), pow_.bitcast(I32), -1.0,
                                        float((254 + exp) * 2 ** 23), ALU.mult, ALU.add)
                last(ins)

            def u_max(j):
                dve.wait_ge(s_u[j % 4], 16 * (j // 4 + 1))
                dve.tensor_reduce(um[:, j:j + 1],
                                  u_raw[:, j % 4, :, :].rearrange("p k m -> p (k m)"), AX_X,
                                  ALU.max, apply_absolute_value=True).then_inc(s_um, 1)

            def u_scale(j):
                dve.wait_ge(s_uma, j + 1)
                power_of_two(um_pow[:, j:j + 1], um_mul[:, j:j + 1], um_all[:, j:j + 1], U_EXP,
                             lambda ins: ins.then_inc(s_umul, 1))
                for b in range(B):
                    dve.tensor_scalar(unscale[:, b, j:j + 1], um_pow[:, j:j + 1],
                                      2.0 ** -(U_EXP + X_EXP), cs_pow[:, b:b + 1],
                                      ALU.mult, ALU.mult).then_inc(s_umul, 1)

            def u_low(j):
                dve.wait_ge(s_uhi, j + 1)
                dve.wait_ge(s_umul, 3 * j + 1)
                flat = lambda t: t.rearrange("p k m -> p (k m)")
                dve.scalar_tensor_tensor(out=flat(u_lo[:, j, :, :]),
                                         in0=flat(u_raw[:, j % 4, :, :]),
                                         scalar=um_mul[:, j:j + 1], in1=flat(u_hi[:, j, :, :]),
                                         op0=ALU.mult, op1=ALU.subtract).then_inc(s_ulo, 1)

            def condition():
                aux_ready(dve, "scale", 0)
                ins = dve.tensor_scalar(cs[:, :, :].rearrange("p k b -> p (k b)"),
                                        bank("scale", 0)[:, 0:KD * B], 1.0, None, ALU.add)
                ins.then_inc(s_cs, 1)
                dve.wait_ge(s_cs, 1)
                dve.tensor_reduce(cs_max[:, :], cs[:, :, :].rearrange("p k b -> p b k"), AX_X,
                                  ALU.max, apply_absolute_value=True).then_inc(s_cm, 1)

            def condition_scale():
                dve.wait_ge(s_cma, 1)
                power_of_two(cs_pow[:, :], cs_mul[:, :], cs_all[:, :], X_EXP, link)
                for b in range(B):
                    link(dve.tensor_scalar(cs_x[:, :, b], cs[:, :, b], cs_mul[:, b:b + 1], None,
                                           ALU.mult))

            def add_squares(i, ks):
                for k in ks:
                    dve.wait_ge(s_sq, KD * i + k + 1)
                    n = (KD - 1) * i + k
                    if k > 1:
                        dve.wait_ge(s_sqr, n - 1)
                    dve.tensor_tensor(work[:, :], work[:, :], tmp[:, k % 2, :], ALU.add)\
                        .then_inc(s_sqr, 1)

            def rsqrt(i):
                aux_ready(dve, "stat", i)
                ins = dve.tensor_scalar(ms[:, :], bank("stat", i)[:, 0:NT], 1.0 / D, EPS_RMS,
                                        ALU.mult, ALU.add)
                ins.then_inc(s_ms, 1)
                dve.wait_ge(s_ms, i + 1)
                if i == 0:
                    dve.wait_ge(s_table, 1)
                a, half, t, y = ms[:, :], ms_half[:, :], rs_t[:, :], rs[:, i % 2, :]
                link(dve.tensor_scalar(half, a, -0.5, None, ALU.mult))
                link(dve.tensor_scalar(t.bitcast(I32), a.bitcast(I32), 1, None,
                                       ALU.logical_shift_right))
                link(dve.tensor_scalar(y.bitcast(I32), t.bitcast(I32), -1.0, float(RSQRT_SEED),
                                       ALU.mult, ALU.add))
                for n in range(NEWTON):
                    link(dve.tensor_tensor(t, y, y, ALU.mult))
                    link(dve.tensor_tensor(t, t, half, ALU.mult))
                    ins = dve.scalar_tensor_tensor(out=y, in0=t, scalar=1.5, in1=y,
                                                   op0=ALU.add, op1=ALU.mult)
                    if n < NEWTON - 1:
                        link(ins)
                ins.then_inc(s_rs, 1)

            def xs(i, k):
                if k == 0:
                    aux_ready(dve, "rs", i)
                    dve.wait_ge(s_sqr, (KD - 1) * (i + 1))
                if k >= 2:
                    dve.wait_ge(s_xlo, KD * i + k - 1)
                dve.scalar_tensor_tensor(
                    out=tmp[:, k % 2, :], in0=bank("rs", i)[:, :],
                    scalar=cs_x[:, k, BATCH[i]:BATCH[i] + 1], in1=x_sb[:, i % 4, k, :],
                    op0=ALU.mult, op1=ALU.mult).then_inc(s_xs, 1)

            def x_low(i, k):
                dve.wait_ge(s_xhi, KD * i + k + 1)
                dve.wait_ge(s_xs, KD * i + k + 1)
                dve.tensor_tensor(x_lo[:, k, :], tmp[:, k % 2, :], x_hi[:, k, :],
                                  ALU.subtract).then_inc(s_xlo, 1)

            def prepare(i, aside={}):
                for k in range(KD):
                    x_low(i, k)
                    if k in aside:
                        aside[k]()
                    if k + 2 < KD:
                        xs(i, k + 2)

            def multiply(p):
                i, j = divmod(p, NP)
                dve.wait_ge(s_val, p + 1)
                dve.wait_ge(s_gelu, p + 1)
                if i == 0:
                    dve.wait_ge(s_umul, 3 * (j + 1))
                else:
                    dve.wait_ge(s_q, p + 1 - NP)
                dve.scalar_tensor_tensor(out=h_sb[:, j, :], in0=up_ps[2 * (p % 2) + 1][:, :],
                                         scalar=unscale[:, BATCH[i], j:j + 1],
                                         in1=gelu[:, p % 2, :], op0=ALU.mult, op1=ALU.mult)\
                    .then_inc(s_h, 1)

            def group_max(i, g):
                c = QG * g
                dve.wait_ge(s_h, NP * i + c + QG)
                src = h_sb[:, c:c + QG, :].rearrange("p c t -> p t c")
                if g == 0:
                    if i:
                        dve.wait_ge(s_ma, i)
                    link(dve.tensor_reduce(hmax[:, :], src, AX_X, ALU.max,
                                           apply_absolute_value=True))
                    return
                if g == 2 and i + 1 < NB:
                    aux_ready(dve, "stat", i + 1)
                link(dve.tensor_reduce(work[:, :], src, AX_X, ALU.max, apply_absolute_value=True))
                ins = dve.tensor_tensor(hmax[:, :], hmax[:, :], work[:, :], ALU.max)
                if g == NP // QG - 1:
                    ins.then_inc(s_m, 1)
                else:
                    ins.then_inc(s_gm, 1)
                    dve.wait_ge(s_gm, 2 * i + g)

            def scales(i):
                dve.wait_ge(s_ma, i + 1)
                link(dve.tensor_scalar(hstep[:, :], work[:, :], EPS_QUANT, 1.0 / 127.0,
                                       ALU.max, ALU.mult))
                link(dve.reciprocal(qscale[:, :], hstep[:, :]))

            def y_scale(i):
                link(dve.tensor_scalar(yscale[:, :], hstep[:, :], wmean[:, 0:1], None, ALU.mult))

            def q_product(i, c):
                h = h_sb[:, c, :]
                dve.tensor_tensor(h, h, qscale[:, :], ALU.mult).then_inc(s_qm, 1)

            def q_round(i, c):
                if c == 0 and i:
                    aux_ready(dve, "y", i - 1, KD - 1)
                dve.wait_ge(s_qm, NP * i + c + 1)
                dve.tensor_scalar(q_sb[:, c, :], h_sb[:, c, :], ROUND, -ROUND, ALU.add,
                                  ALU.add).then_inc(s_q, 1)

            def residual_product(i, k):
                if i == NB - 1:
                    dve.wait_ge(s_last, k + 1)
                    y = up_ps[k][:, :]
                else:
                    aux_ready(dve, "y", i, k)
                    y = bank("y", i, k)[:, :]
                dve.tensor_tensor(y, y, yscale[:, :], ALU.mult).then_inc(s_y, 1)
                return y

            def residual(i, ks):
                y = residual_product(i, ks[0])
                for k in ks:
                    ahead = residual_product(i, k + 1) if k + 1 in ks else None
                    xk = on_chip("x", i)[:, k, :]
                    dve.wait_ge(s_y, KD * i + k + 1)
                    dve.tensor_tensor(xk, y, xk, ALU.add).then_inc(s_x1, 1)
                    y = ahead

            def finish(i, k):
                aux_ready(dve, "up", i, k)
                xk = on_chip("back" if i in PARKED else "x", i)[:, k, :]
                dve.scalar_tensor_tensor(out=xk, in0=bank("up", i, k)[:, :],
                                         scalar=bu_sb[:, k:k + 1], in1=xk,
                                         op0=ALU.add, op1=ALU.add).then_inc(s_out, 1)

            def down_mean():
                dve.wait_ge(s_dabs, 8)
                dve.tensor_reduce(dsum[:, :], dabs[:, :], AX_X, ALU.add).then_inc(s_dsum, 1)

            def down_scale():
                dve.wait_ge(s_dsuma, 1)
                link(dve.tensor_scalar(wmean[:, :], dsum_all[:, :], 1.0 / (D * FF), 1e-5,
                                       ALU.mult, ALU.max))
                link(dve.reciprocal(wmul[:, :], wmean[:, :]))

            def down_quantise(n):
                dve.wait_ge(s_d[n % 2], 16 * (4 + n // 2 + 1))
                raw = d_raw[:, n % 2, :]
                link(dve.tensor_scalar(raw, raw, wmul[:, 0:1], 1.0, ALU.mult, ALU.min))
                link(dve.tensor_scalar(raw, raw, -1.0, ROUND, ALU.max, ALU.add))
                dve.tensor_scalar(wq[:, 2 * n:2 * n + 2, :].rearrange("p c d -> p (c d)"), raw,
                                  ROUND, None, ALU.subtract, saturate=False).then_inc(s_wq, 1)

            def assemble():
                for n in range(2):
                    dve.wait_ge(s_move[n], 16 * B * NG // 2)
                for n, dst in ((0, l1_wd[:, :, :, :].rearrange("p b k n -> p b (k n)")),
                               (1, l1_wu[:, :, :])):
                    slot = (2 * NG + n) % 4
                    dve.wait_ge(s_w[slot], 16 * (NG // 2) + 32)
                    for b in range(B):
                        link(dve.tensor_tensor(dst[:, b, :], dst[:, b, :],
                                               w_ring[:, slot, 512:1024], ALU.add))
                        dve.scalar_tensor_tensor(out=dst[:, b, :], in0=dst[:, b, :],
                                                 scalar=DELTA_SCALE, in1=w_ring[:, slot, 0:512],
                                                 op0=ALU.mult, op1=ALU.add).then_inc(s_l1w, 1)

            dve.memset(cond_sb[:, :], 0.0).then_inc(s_zero, 1)
            add_squares(0, range(1, KD))
            condition()
            u_max(0)
            condition_scale()
            u_scale(0)
            rsqrt(0)
            u_low(0)
            xs(0, 0)
            xs(0, 1)
            prepare(0, {0: lambda: u_max(1), 2: lambda: u_scale(1)})
            for p in range(STEPS):
                i, j = divmod(p, NP)
                if i == 0 and j + 1 < NP:
                    u_low(j + 1)
                    if j + 2 < NP:
                        u_max(j + 2)
                        u_scale(j + 2)
                if i:
                    if j == 0:
                        q_product(i - 1, 0)
                    if j + 1 < NP:
                        q_product(i - 1, j + 1)
                    q_round(i - 1, j)
                if j == NP - 1 and i + 1 < NB:
                    xs(i + 1, 0)
                    xs(i + 1, 1)
                multiply(p)
                for n, step in ADAPTER_STEP.items():
                    if p == step + 2:
                        for k in range(KD):
                            finish(n, k)
                if 1 <= j - SQUARES < KD and i + 1 < NB:
                    add_squares(i + 1, (j - SQUARES,))
                if j == STAT_PAIR + 1 and i + 1 < NB:
                    rsqrt(i + 1)
                if j in GROUP_MAX:
                    group_max(i, GROUP_MAX.index(j))
                if p == NP:
                    down_scale()
                if i == 1 and j < 8:
                    down_quantise(j)
                if p == ASSEMBLE:
                    assemble()
                if j == NP - 1:
                    if i + 1 < NB:
                        prepare(i + 1)
                    if i == 0:
                        down_mean()
                    group_max(i, NP // QG - 1)
                    if i == 0:
                        scales(i)
                    else:
                        y_scale(i - 1)
                        residual(i - 1, range(0, 1))
                        scales(i)
                        residual(i - 1, range(1, KD))
            i = NB - 1
            q_product(i, 0)
            for c in range(NP):
                if c + 1 < NP:
                    q_product(i, c + 1)
                q_round(i, c)
                for a in range(2):
                    half = c - 5 - 4 * a
                    if half in (0, 1):
                        finish(TAIL[0][a], 2 * half)
                        finish(TAIL[0][a], 2 * half + 1)
            y_scale(i)
            residual(i, range(KD))
            for n in TAIL[1]:
                for k in range(KD):
                    finish(n, k)


def kernel(x, cond_256, L0_cond_norm_w, L0_cond_up_w, L0_cond_down_w, L1_cond_Wd, L1_cond_bd,
           L1_cond_Wu, L1_cond_bu, L1_cond_Wdd, L1_cond_bdd, L1_cond_Wdu, L1_cond_bdu):
    import concourse.bacc as bacc
    from concourse.bass_utils import run_bass_kernel_spmd

    lay = {
        "x": np.asarray(x).reshape(B * S, KD, P).transpose(2, 1, 0),
        "cond": np.asarray(cond_256).T,
        "norm_w": np.asarray(L0_cond_norm_w).T,
        "up_w": np.asarray(L0_cond_up_w).reshape(2, NP, P, KD, P).transpose(1, 4, 3, 0, 2)
            .reshape(NP, P, KD, UW),
        "down_w": np.asarray(L0_cond_down_w).reshape(D, NP // 2, 2, P).transpose(1, 3, 2, 0)
            .reshape(NP // 2, P, 2 * D),
        "Wd": np.asarray(L1_cond_Wd).reshape(BN, KD, P).transpose(2, 1, 0).reshape(P, KD * BN),
        "bd": np.asarray(L1_cond_bd).reshape(BN, 1),
        "Wu": np.asarray(L1_cond_Wu).T,
        "bu": np.asarray(L1_cond_bu).reshape(KD, P).T,
        "Wdd": np.asarray(L1_cond_Wdd).reshape(BN, KD, 4, NG_HALF, H).transpose(3, 4, 2, 1, 0)
            .reshape(NG_HALF, H, 2, 1024).transpose(0, 2, 1, 3).reshape(NG, H, 1024),
        "bdd": np.asarray(L1_cond_bdd).reshape(BN, KD, P).transpose(2, 1, 0).reshape(P, KD * BN),
        "Wdu": np.asarray(L1_cond_Wdu).reshape(D, 4, NG_HALF, H).transpose(2, 3, 1, 0)
            .reshape(NG_HALF, H, 2, 1024).transpose(0, 2, 1, 3).reshape(NG, H, 1024),
        "bdu": np.asarray(L1_cond_bdu).reshape(D, BN).T,
    }
    nc = bacc.Bacc("TRN2", target_bir_lowering=False, num_devices=1)
    arrays, args = {}, []
    for name, a in lay.items():
        a = np.ascontiguousarray(a)
        arrays[f"in_{name}"] = a
        args.append(nc.dram_tensor(f"in_{name}", a.shape, mybir.dt.from_np(a.dtype),
                                   kind="ExternalInput").ap())
    args.append(nc.dram_tensor("out", (P, KD, B * S), F32, kind="ExternalOutput").ap())
    build(nc, *args)
    got = run_bass_kernel_spmd(nc, [arrays], core_ids=[0]).results[0]["out"]
    return np.ascontiguousarray(got.transpose(2, 1, 0)).reshape(B, S, D)
```
